# Optimizing a Trainium2 kernel written in Bass

```python
import numpy as np
import jax
import jax.numpy as jnp

def _softmax(x, axis=-1):
    return jax.nn.softmax(x, axis=axis)

def _gelu(x):
    return jax.nn.gelu(x, approximate=True)

def _silu(x):
    return jax.nn.silu(x)

def _sigmoid(x):
    return jax.nn.sigmoid(x)

def _layernorm(x, axis=-1, eps=1e-05):
    m = jnp.mean(x, axis=axis, keepdims=True)
    v = jnp.var(x, axis=axis, keepdims=True)
    return (x - m) / jnp.sqrt(v + eps)

def _scatter_add(tgt, idx, src, axis=0):
    return tgt.at[idx].add(src)

def _segment_sum(src, seg, n):
    return jax.ops.segment_sum(src, seg, n)
kernel_name = 'mk_early_fusion_d2_tok_img1024_r4_f9e221'

def setup_inputs(seed: int=0):
    np.random.seed(seed)
    _w = jnp.asarray

    def _rec_inputs():
        import jax
        import jax.numpy as jnp
        _rk = jax.random.key(seed)
        x = -0.00016672 + 0.999947 * jax.random.normal(jax.random.fold_in(_rk, 1), (64, 3, 96, 96), jnp.float32)
        txt = 2.71836e-05 + 0.999386 * jax.random.normal(jax.random.fold_in(_rk, 2), (64, 32, 256), jnp.float32)
        return (x, txt)
    x, txt = _rec_inputs()

    def _L0_tok_setup():
        import jax, jax.numpy as jnp
        import numpy as np
        IMG = 96
        PATCH = 16
        C_IN = 3
        EMBED = 256
        NPH = IMG // PATCH
        NUM_PATCHES = NPH * NPH
        PATCH_DIM = PATCH * PATCH * C_IN
        key = jax.random.key(seed)
        k_x, k_w, k_b, k_cls, k_pos = jax.random.split(key, 5)
        x = jax.random.normal(k_x, (64, C_IN, IMG, IMG), dtype=jnp.float32)
        W = jax.random.normal(k_w, (EMBED, PATCH_DIM), dtype=jnp.float32) * (1.0 / np.sqrt(PATCH_DIM))
        b = jax.random.normal(k_b, (EMBED,), dtype=jnp.float32) * 0.01
        cls_token = jax.random.normal(k_cls, (1, 1, EMBED), dtype=jnp.float32) * 0.02
        pos_embed = jax.random.normal(k_pos, (1, NUM_PATCHES + 1, EMBED), dtype=jnp.float32) * 0.02
        return {'x': x, 'W': W, 'b': b, 'cls_token': cls_token, 'pos_embed': pos_embed}
    _L0_tok_all = _L0_tok_setup()
    _L0_tok_in = {k: v for k, v in _L0_tok_all.items() if k in ('W', 'b', 'cls_token', 'pos_embed')}
    del _L0_tok_all

    def _L0_attn_setup():
        import jax, jax.numpy as jnp
        import numpy as np
        B, T, C = (8, 512, 256)

        def _rotate(z, cos_a, sin_a):
            b, t, c = z.shape
            z = z.reshape(b, t, c // 2, 2)
            z0, z1 = (z[..., 0], z[..., 1])
            r0 = cos_a * z0 + sin_a * z1
            r1 = -sin_a * z0 + cos_a * z1
            return jnp.stack([r0, r1], axis=-1).reshape(b, t, c)
        key = jax.random.key(seed)
        ks = jax.random.split(key, 9)
        s = 1.0 / np.sqrt(C)
        return {'x': jax.random.normal(ks[0], (B, T, C), dtype=jnp.float32), 'Wk': jax.random.uniform(ks[1], (C, C), jnp.float32, -s, s), 'bk': jax.random.uniform(ks[2], (C,), jnp.float32, -s, s), 'Wq': jax.random.uniform(ks[3], (C, C), jnp.float32, -s, s), 'bq': jax.random.uniform(ks[4], (C,), jnp.float32, -s, s), 'Wv': jax.random.uniform(ks[5], (C, C), jnp.float32, -s, s), 'bv': jax.random.uniform(ks[6], (C,), jnp.float32, -s, s), 'Wp': jax.random.uniform(ks[7], (C, C), jnp.float32, -s, s), 'bp': jax.random.uniform(ks[8], (C,), jnp.float32, -s, s)}
    _L0_attn_all = _L0_attn_setup()
    _L0_attn_in = {k: v for k, v in _L0_attn_all.items() if k in ('Wk', 'bk', 'Wq', 'bq', 'Wv', 'bv', 'Wp', 'bp')}
    del _L0_attn_all

    def _L0_ffn_setup():
        import jax, jax.numpy as jnp
        import numpy as np
        EPS = 1e-05

        def _quantize(W):
            gamma = jnp.mean(jnp.abs(W))
            return jnp.clip(jnp.round(W / (gamma + EPS)), -1.0, 1.0)
        key = jax.random.key(seed)
        k_x, k_w1, k_b1, k_w2, k_b2 = jax.random.split(key, 5)
        n_embd = 256
        d_ff = 4 * n_embd
        B, S = (4, 1024)
        bound1 = 1.0 / np.sqrt(n_embd)
        bound2 = 1.0 / np.sqrt(d_ff)
        x = jax.random.normal(k_x, (B, S, n_embd), dtype=jnp.float32)
        W1 = jax.random.uniform(k_w1, (d_ff, n_embd), jnp.float32, -bound1, bound1)
        b1 = jax.random.uniform(k_b1, (d_ff,), jnp.float32, -bound1, bound1)
        W2 = jax.random.uniform(k_w2, (n_embd, d_ff), jnp.float32, -bound2, bound2)
        b2 = jax.random.uniform(k_b2, (n_embd,), jnp.float32, -bound2, bound2)
        return {'x': x, 'W1': W1, 'b1': b1, 'W2': W2, 'b2': b2}
    _L0_ffn_all = _L0_ffn_setup()
    _L0_ffn_in = {k: v for k, v in _L0_ffn_all.items() if k in ('W1', 'b1', 'W2', 'b2')}
    del _L0_ffn_all

    def _L1_attn_setup():
        import jax, jax.numpy as jnp
        import numpy as np

        def _reference_tuple_inner(x, B_w, C_w, log_A, D_param):
            A = jnp.exp(log_A)
            x_proj = jnp.einsum('bld,nd->bln', x, B_w)

            def step(h, u):
                h = A * h + u
                return (h, h)
            h0 = jnp.zeros((x.shape[0], B_w.shape[0]), x.dtype)
            _, hs = jax.lax.scan(step, h0, jnp.swapaxes(x_proj, 0, 1))
            y = jnp.einsum('lbn,dn->bld', hs, C_w)
            y = y + x * D_param
            last = x_proj[:, -1, :]
            final_state = jnp.broadcast_to(last.mean(axis=0, keepdims=True), last.shape)
            return (y, final_state)
        key = jax.random.key(seed)
        kx, kb, kc, ka, kd = jax.random.split(key, 5)
        B, L, D, N = (8, 1024, 256, 128)
        x = jax.random.normal(kx, (B, L, D), jnp.float32)
        B_w = jax.random.normal(kb, (N, D), jnp.float32) * 0.01
        C_w = jax.random.normal(kc, (D, N), jnp.float32)
        log_A = -jax.random.uniform(ka, (N,), jnp.float32) * 3.0 - 0.1
        D_param = jax.random.normal(kd, (D,), jnp.float32)
        return dict(x=x, B_w=B_w, C_w=C_w, log_A=log_A, D_param=D_param)
    _L1_attn_all = _L1_attn_setup()
    _L1_attn_in = {k: v for k, v in _L1_attn_all.items() if k in ('B_w', 'C_w', 'log_A', 'D_param')}
    del _L1_attn_all

    def _L1_ffn_setup():
        import jax, jax.numpy as jnp
        import numpy as np
        B, L, M = (4, 512, 256)
        G, E = (8, 8)
        CAP_FACTOR = 2.0

        def _ffn_size(m, widening=8.0):
            f = int(widening * m) * 2 // 3
            return f + (8 - f) % 8
        H = _ffn_size(M)

        def _gating_top2(logits, C):
            Gd, Sd, Ed = logits.shape
            raw = jax.nn.softmax(logits, axis=-1)
            idx1 = jnp.argmax(raw, axis=-1)
            m1 = jax.nn.one_hot(idx1, Ed, dtype=logits.dtype)
            gate1 = jnp.sum(raw * m1, axis=-1)
            rest = raw * (1.0 - m1)
            idx2 = jnp.argmax(rest, axis=-1)
            m2 = jax.nn.one_hot(idx2, Ed, dtype=logits.dtype)
            gate2 = jnp.sum(rest * m2, axis=-1)
            p1 = jnp.cumsum(m1, axis=-2) - m1
            m1 = m1 * (p1 < C).astype(m1.dtype)
            p1 = jnp.sum(p1 * m1, axis=-1)
            m1_flat = jnp.sum(m1, axis=-1)
            m1_count = jnp.sum(m1, axis=-2)
            p2 = jnp.cumsum(m2, axis=-2) - m2 + m1_count[:, None, :]
            m2 = m2 * (p2 < C).astype(m2.dtype)
            p2 = jnp.sum(p2 * m2, axis=-1)
            m2_flat = jnp.sum(m2, axis=-1)
            gate1 = gate1 * m1_flat
            gate2 = gate2 * m2_flat
            c1 = (gate1[..., None] * jax.nn.one_hot(idx1, Ed, dtype=jnp.float32))[..., None] * jax.nn.one_hot(p1.astype(jnp.int32), C, dtype=jnp.float32)[:, :, None, :]
            c2 = (gate2[..., None] * jax.nn.one_hot(idx2, Ed, dtype=jnp.float32))[..., None] * jax.nn.one_hot(p2.astype(jnp.int32), C, dtype=jnp.float32)[:, :, None, :]
            combine = (c1 + c2).astype(logits.dtype)
            dispatch = (combine != 0).astype(logits.dtype)
            return (dispatch, combine)
        key = jax.random.key(seed)
        k0, k1, k2, k3, k4 = jax.random.split(key, 5)
        return {'inputs': jax.random.normal(k0, (B, L, M), jnp.float32), 'router_w': jax.random.normal(k1, (M, E), jnp.float32) * 0.02, 'w0_kernel': jax.random.normal(k2, (E, M, H), jnp.float32) * 0.02, 'w1_kernel': jax.random.normal(k3, (E, M, H), jnp.float32) * 0.02, 'wo_kernel': jax.random.normal(k4, (E, H, M), jnp.float32) * 0.02}
    _L1_ffn_all = _L1_ffn_setup()
    _L1_ffn_in = {k: v for k, v in _L1_ffn_all.items() if k in ('router_w', 'w0_kernel', 'w1_kernel', 'wo_kernel')}
    del _L1_ffn_all
    return {'x': x, 'txt': txt, 'L0_tok_W': _L0_tok_in['W'], 'L0_tok_b': _L0_tok_in['b'], 'L0_tok_cls_token': _L0_tok_in['cls_token'], 'L0_tok_pos_embed': _L0_tok_in['pos_embed'], 'L0_attn_Wk': _L0_attn_in['Wk'], 'L0_attn_bk': _L0_attn_in['bk'], 'L0_attn_Wq': _L0_attn_in['Wq'], 'L0_attn_bq': _L0_attn_in['bq'], 'L0_attn_Wv': _L0_attn_in['Wv'], 'L0_attn_bv': _L0_attn_in['bv'], 'L0_attn_Wp': _L0_attn_in['Wp'], 'L0_attn_bp': _L0_attn_in['bp'], 'L0_ffn_W1': _L0_ffn_in['W1'], 'L0_ffn_b1': _L0_ffn_in['b1'], 'L0_ffn_W2': _L0_ffn_in['W2'], 'L0_ffn_b2': _L0_ffn_in['b2'], 'L1_attn_B_w': _L1_attn_in['B_w'], 'L1_attn_C_w': _L1_attn_in['C_w'], 'L1_attn_log_A': _L1_attn_in['log_A'], 'L1_attn_D_param': _L1_attn_in['D_param'], 'L1_ffn_router_w': _L1_ffn_in['router_w'], 'L1_ffn_w0_kernel': _L1_ffn_in['w0_kernel'], 'L1_ffn_w1_kernel': _L1_ffn_in['w1_kernel'], 'L1_ffn_wo_kernel': _L1_ffn_in['wo_kernel']}

def reference(x, txt, L0_tok_W, L0_tok_b, L0_tok_cls_token, L0_tok_pos_embed, L0_attn_Wk, L0_attn_bk, L0_attn_Wq, L0_attn_bq, L0_attn_Wv, L0_attn_bv, L0_attn_Wp, L0_attn_bp, L0_ffn_W1, L0_ffn_b1, L0_ffn_W2, L0_ffn_b2, L1_attn_B_w, L1_attn_C_w, L1_attn_log_A, L1_attn_D_param, L1_ffn_router_w, L1_ffn_w0_kernel, L1_ffn_w1_kernel, L1_ffn_wo_kernel):
    import jax
    import jax.numpy as jnp

    def _L0_tok_ref(x, W, b, cls_token, pos_embed):
        import jax, jax.numpy as jnp
        import numpy as np
        IMG = 96
        PATCH = 16
        C_IN = 3
        EMBED = 256
        NPH = IMG // PATCH
        NUM_PATCHES = NPH * NPH
        PATCH_DIM = PATCH * PATCH * C_IN
        B, C, H, Wd = x.shape
        nph, npw = (H // PATCH, Wd // PATCH)
        patches = x.reshape(B, C, nph, PATCH, npw, PATCH)
        patches = patches.transpose(0, 2, 4, 1, 3, 5)
        patches = patches.reshape(B, nph * npw, C * PATCH * PATCH)
        proj = jnp.einsum('bnd,ed->bne', patches, W) + b
        cls = jnp.broadcast_to(cls_token, (B, 1, cls_token.shape[-1]))
        out = jnp.concatenate([cls, proj], axis=1) + pos_embed
        return out

    def _L0_attn_ref(x, Wk, bk, Wq, bq, Wv, bv, Wp, bp):
        import jax, jax.numpy as jnp
        import numpy as np
        B, T, C = (8, 512, 256)

        def _rotate(z, cos_a, sin_a):
            b, t, c = z.shape
            z = z.reshape(b, t, c // 2, 2)
            z0, z1 = (z[..., 0], z[..., 1])
            r0 = cos_a * z0 + sin_a * z1
            r1 = -sin_a * z0 + cos_a * z1
            return jnp.stack([r0, r1], axis=-1).reshape(b, t, c)
        b, t, c = x.shape
        half = c // 2
        k = x @ Wk + bk
        q = x @ Wq + bq
        v = x @ Wv + bv
        angle = jnp.outer(jnp.arange(t, dtype=jnp.float32), jnp.arange(half, dtype=jnp.float32))[::-1]
        cos_a = jnp.cos(angle)
        sin_a = jnp.sin(angle)
        k = _rotate(k, cos_a, sin_a)
        q = _rotate(q, cos_a, sin_a)
        wei = jnp.einsum('bic,bjc->bij', k, q) * c ** (-0.5)
        mask = jnp.tril(jnp.ones((t, t), dtype=bool))
        wei = jnp.where(mask, wei, -jnp.inf)
        wei = jax.nn.softplus(wei)
        out = wei @ v
        out = out @ Wp + bp
        return out

    def _L0_ffn_ref(x, W1, b1, W2, b2):
        import jax, jax.numpy as jnp
        import numpy as np
        EPS = 1e-05

        def _quantize(W):
            gamma = jnp.mean(jnp.abs(W))
            return jnp.clip(jnp.round(W / (gamma + EPS)), -1.0, 1.0)
        Wq1 = _quantize(W1)
        Wq2 = _quantize(W2)
        h = jax.nn.relu(jnp.einsum('bsd,fd->bsf', x, Wq1) + b1)
        out = jnp.einsum('bsf,df->bsd', h, Wq2) + b2
        return out

    def _L1_attn_ref(x, B_w, C_w, log_A, D_param):
        import jax, jax.numpy as jnp
        import numpy as np

        def _reference_tuple_inner(x, B_w, C_w, log_A, D_param):
            A = jnp.exp(log_A)
            x_proj = jnp.einsum('bld,nd->bln', x, B_w)

            def step(h, u):
                h = A * h + u
                return (h, h)
            h0 = jnp.zeros((x.shape[0], B_w.shape[0]), x.dtype)
            _, hs = jax.lax.scan(step, h0, jnp.swapaxes(x_proj, 0, 1))
            y = jnp.einsum('lbn,dn->bld', hs, C_w)
            y = y + x * D_param
            last = x_proj[:, -1, :]
            final_state = jnp.broadcast_to(last.mean(axis=0, keepdims=True), last.shape)
            return (y, final_state)
        return _reference_tuple_inner(x, B_w, C_w, log_A, D_param)[0]

    def _L1_ffn_ref(inputs, router_w, w0_kernel, w1_kernel, wo_kernel):
        import jax, jax.numpy as jnp
        import numpy as np
        B, L, M = (4, 512, 256)
        G, E = (8, 8)
        CAP_FACTOR = 2.0

        def _ffn_size(m, widening=8.0):
            f = int(widening * m) * 2 // 3
            return f + (8 - f) % 8
        H = _ffn_size(M)

        def _gating_top2(logits, C):
            Gd, Sd, Ed = logits.shape
            raw = jax.nn.softmax(logits, axis=-1)
            idx1 = jnp.argmax(raw, axis=-1)
            m1 = jax.nn.one_hot(idx1, Ed, dtype=logits.dtype)
            gate1 = jnp.sum(raw * m1, axis=-1)
            rest = raw * (1.0 - m1)
            idx2 = jnp.argmax(rest, axis=-1)
            m2 = jax.nn.one_hot(idx2, Ed, dtype=logits.dtype)
            gate2 = jnp.sum(rest * m2, axis=-1)
            p1 = jnp.cumsum(m1, axis=-2) - m1
            m1 = m1 * (p1 < C).astype(m1.dtype)
            p1 = jnp.sum(p1 * m1, axis=-1)
            m1_flat = jnp.sum(m1, axis=-1)
            m1_count = jnp.sum(m1, axis=-2)
            p2 = jnp.cumsum(m2, axis=-2) - m2 + m1_count[:, None, :]
            m2 = m2 * (p2 < C).astype(m2.dtype)
            p2 = jnp.sum(p2 * m2, axis=-1)
            m2_flat = jnp.sum(m2, axis=-1)
            gate1 = gate1 * m1_flat
            gate2 = gate2 * m2_flat
            c1 = (gate1[..., None] * jax.nn.one_hot(idx1, Ed, dtype=jnp.float32))[..., None] * jax.nn.one_hot(p1.astype(jnp.int32), C, dtype=jnp.float32)[:, :, None, :]
            c2 = (gate2[..., None] * jax.nn.one_hot(idx2, Ed, dtype=jnp.float32))[..., None] * jax.nn.one_hot(p2.astype(jnp.int32), C, dtype=jnp.float32)[:, :, None, :]
            combine = (c1 + c2).astype(logits.dtype)
            dispatch = (combine != 0).astype(logits.dtype)
            return (dispatch, combine)
        Bb, Ll, Mm = inputs.shape
        S = Bb * Ll // G
        x = inputs.reshape(G, S, Mm)
        logits = jnp.einsum('GSM,ME->GSE', x, router_w)
        cap = int(CAP_FACTOR * S / E)
        C = (cap + 3) // 4 * 4
        dispatch, combine = _gating_top2(logits, C)
        expert_inputs = jnp.einsum('GSEC,GSM->EGCM', dispatch, x)
        layer_w0 = jnp.einsum('EGCM,EMH->EGCH', expert_inputs, w0_kernel)
        layer_w1 = jnp.einsum('EGCM,EMH->EGCH', expert_inputs, w1_kernel)
        hidden = jax.nn.gelu(layer_w0, approximate=True) * layer_w1
        expert_outputs = jnp.einsum('EGCH,EHM->EGCM', hidden, wo_kernel)
        out = jnp.einsum('EGCM,GSEC->GSM', expert_outputs, combine)
        return out.reshape(Bb, Ll, Mm)
    h = _L0_tok_ref(x, L0_tok_W, L0_tok_b, L0_tok_cls_token, L0_tok_pos_embed)
    h = jnp.concatenate([h, txt], axis=1)
    h = h + _L0_attn_ref(_layernorm(h, axis=-1), L0_attn_Wk, L0_attn_bk, L0_attn_Wq, L0_attn_bq, L0_attn_Wv, L0_attn_bv, L0_attn_Wp, L0_attn_bp)
    h = h + _L0_ffn_ref(_layernorm(h, axis=-1), L0_ffn_W1, L0_ffn_b1, L0_ffn_W2, L0_ffn_b2)
    h = h + _L1_attn_ref(_layernorm(h, axis=-1), L1_attn_B_w, L1_attn_C_w, L1_attn_log_A, L1_attn_D_param)
    h = h + _L1_ffn_ref(_layernorm(h, axis=-1), L1_ffn_router_w, L1_ffn_w0_kernel, L1_ffn_w1_kernel, L1_ffn_wo_kernel)
    return h

_drawn_inputs = setup_inputs


def setup_inputs(seed=0):
    import zlib

    import numpy as np

    out = dict(_drawn_inputs(seed))
    spreads = {}
    factors = {'L0_attn_bk': 5.131,
     'L0_attn_bq': 5.409,
     'L0_ffn_b1': 8.0,
     'L0_ffn_b2': 200.0,
     'L1_attn_B_w': 4.498,
     'L1_attn_C_w': 3.912,
     'L1_attn_log_A': 194.32,
     'L1_attn_D_param': 8.0,
     'L1_ffn_router_w': 8.0,
     'L1_ffn_w0_kernel': 8.0,
     'L1_ffn_w1_kernel': 8.0,
     'L1_ffn_wo_kernel': 8.0}
    for name, (base, spread) in spreads.items():
        noise = np.random.default_rng([zlib.crc32(name.encode()), seed]).standard_normal(out[name].shape)
        drawn = base * np.exp(spread * noise) if base else spread * noise
        out[name] = jnp.asarray(drawn.astype(out[name].dtype))
    for name, factor in factors.items():
        out[name] = (out[name] * factor).astype(out[name].dtype)
    return out
```

```python
from contextlib import ExitStack

import concourse.bass as bass
from concourse import mybir

F32 = mybir.dt.float32
F32R = mybir.dt.float32r
BF16 = mybir.dt.bfloat16
U32 = mybir.dt.uint32
ALU = mybir.AluOpType
ACT = mybir.ActivationFunctionType
AX = mybir.AxisListType.X

P = 128
B = 64
NPATCH = 36
NTXT = 32
L = 1 + NPATCH + NTXT
D = 256
KD = D // P
NTOK = B * L
SEQ = 4
T = SEQ * L
NCH = B // SEQ
TT = 92
TPC = T // TT
NTILE = NTOK // TT
G = 8
TPG = NTILE // G
GSEQ = B // G
PD = 768
KP = PD // P
GP = GSEQ * NPATCH
F = 1024
KF = F // P
NS = 128
E = 8
CAP = 140
H = 1368
HT = [(i * P, min(P, H - i * P)) for i in range(-(-H // P))]
NH = len(HT)
SLOTS = G * CAP
CHUNKS = [(0, 374), (374, 374), (748, 372)]
NJ = len(CHUNKS)
NC = CHUNKS[0][1]
ST = 3
NROW = E * SLOTS
ROW = D + 1 + E
BIG = 65536.0
EPS = 1e-5
QEPS = 1e-5
SCALE = float(D) ** -0.5
MASKED = -1e30
ROUND = 12582912.0


def slot_tiles(n):
    a = -(-n // ST)
    return [(0, a), (a, a), (2 * a, n - 2 * a)]


SMAX = slot_tiles(NC)[0][1]


def fixed(c):
    return isinstance(c, int)


def fusion_kernel(nc, patches, txt, cls, pos0, pos, tok_b, w_patch, w_k, w_q, w_vT, w_p, b_k, b_q, b_v, b_p,
                  rot_cos, rot_sin, mask, w1T, b1, w2T, b2, b_wT, c_wT, log_a, d_param, w_r,
                  w0, w1, wo, ident, upper, tokno, slotbase, revno, out):
    ctx = ExitStack()
    with ctx:
        def sem(name):
            return ctx.enter_context(nc.semaphore(name))

        def sbuf(stack, name, shape, dt=F32):
            return stack.enter_context(nc.sbuf_tensor(name, shape, dt))

        xrows = nc.dram_tensor("xrows", (NROW, ROW), F32).ap()

        idt = sbuf(ctx, "idt", [P, P])
        wst = sbuf(ctx, "wst", [P, 2 * KD, H])
        wost = sbuf(ctx, "wost", [P, NH, D])

        pre = ExitStack()
        h = sbuf(pre, "h", [TT, NTILE, D])
        xt = sbuf(pre, "xt", [TT, TPC, D])
        xhi = [sbuf(pre, f"xhi{u}", [P, KD, T], F32R) for u in range(2)]
        xlo = [sbuf(pre, f"xlo{u}", [P, KD, T], F32R) for u in range(2)]
        oT = sbuf(pre, "oT", [P, KD, T])
        st = sbuf(pre, "st", [TT, TPC, 6])
        mv = sbuf(pre, "mv", [TT, TPC, 2])
        ve = sbuf(pre, "ve", [TT, TPC])
        rstd = sbuf(pre, "rstd", [TT, TPC])
        mhalf = sbuf(pre, "mhalf", [TT, TPC])
        epst = sbuf(pre, "epst", [TT, TPC])
        w1st = sbuf(pre, "w1st", [P, KD, F])
        w1q = sbuf(pre, "w1q", [P, KD, F], F32R)
        w2q = sbuf(pre, "w2q", [P, KF, D], F32R)
        bhi = sbuf(pre, "bhi", [P, KD, NS], F32R)
        blo = sbuf(pre, "blo", [P, KD, NS], F32R)
        chi = sbuf(pre, "chi", [P, D], F32R)
        clo = sbuf(pre, "clo", [P, D], F32R)
        dmat = sbuf(pre, "dmat", [P, KD, P])
        dhi = sbuf(pre, "dhi", [P, KD, P], F32R)
        dlo = sbuf(pre, "dlo", [P, KD, P], F32R)
        at = sbuf(pre, "at", [P, L])
        lat = sbuf(pre, "lat", [P, 1])
        dpt = sbuf(pre, "dpt", [P, KD])
        bkt = sbuf(pre, "bkt", [P, KD])
        bqt = sbuf(pre, "bqt", [P, KD])
        bvt = sbuf(pre, "bvt", [P, KD])
        bpt = sbuf(pre, "bpt", [P, KD])
        b1t = sbuf(pre, "b1t", [P, KF])
        b2t = sbuf(pre, "b2t", [P, KD])
        onesf = sbuf(pre, "onesf", [P, P])
        gsum = sbuf(pre, "gsum", [P, 2])
        gam = sbuf(pre, "gam", [P, 2])
        ginv = sbuf(pre, "ginv", [P, 2])
        wr = sbuf(pre, "wr", [P, KD, E])
        base = sbuf(pre, "base", [TT, G, 2 * E])
        rev = sbuf(pre, "rev", [TT, E])
        upf = sbuf(pre, "upf", [TT, TT])
        up = sbuf(pre, "up", [TT, TT], BF16)
        ones = sbuf(pre, "ones", [TT, TT], BF16)
        tno = sbuf(pre, "tno", [TT, NTILE])

        layers = ExitStack()
        khi = sbuf(layers, "khi", [P, KD, D], F32R)
        klo = sbuf(layers, "klo", [P, KD, D], F32R)
        qhi = sbuf(layers, "qhi", [P, KD, D], F32R)
        qlo = sbuf(layers, "qlo", [P, KD, D], F32R)
        vhi = sbuf(layers, "vhi", [P, KD, D], F32R)
        vlo = sbuf(layers, "vlo", [P, KD, D], F32R)
        bvx = sbuf(layers, "bvx", [P, KD, L])
        bvp = sbuf(layers, "bvp", [L, D])
        cosT = sbuf(layers, "cosT", [P, L])
        sinT = sbuf(layers, "sinT", [P, KD, L])
        msk = sbuf(layers, "msk", [L, L])

        embed_ = ExitStack()
        pst = [sbuf(embed_, f"pst{u}", [P, KP, GP]) for u in range(2)]
        ehi = [sbuf(embed_, f"ehi{u}", [P, KP, GP], F32R) for u in range(2)]
        elo = [sbuf(embed_, f"elo{u}", [P, KP, GP], F32R) for u in range(2)]
        emb = [sbuf(embed_, f"emb{u}", [P, KD, GSEQ, L]) for u in range(2)]
        wphi = sbuf(embed_, "wphi", [P, KP, D], F32R)
        wplo = sbuf(embed_, "wplo", [P, KP, D], F32R)
        posb = sbuf(embed_, "posb", [P, KD, NPATCH])
        clst = sbuf(embed_, "clst", [P, KD])
        pos0t = sbuf(embed_, "pos0t", [P, KD])
        tokbt = sbuf(embed_, "tokbt", [P, KD])
        embed_.close()

        zk = sbuf(layers, "zk", [P, KD, T])
        zq = sbuf(layers, "zq", [P, KD, T])
        ra = sbuf(layers, "ra", [P, KD, T])
        rb = sbuf(layers, "rb", [P, KD, T])
        kR = sbuf(layers, "kR", [P, KD, T])
        qR = sbuf(layers, "qR", [P, KD, T])
        vp = [sbuf(layers, f"vp{u}", [L, SEQ, D]) for u in range(2)]
        wm = sbuf(layers, "wm", [L, T])
        wa = sbuf(layers, "wa", [L, T])
        we = sbuf(layers, "we", [L, T])
        wl = sbuf(layers, "wl", [L, T])
        wp = [sbuf(layers, f"wp{u}", [L, T]) for u in range(2)]
        hhi = sbuf(layers, "hhi", [P, KF, T], F32R)
        hlo = sbuf(layers, "hlo", [P, KF, T], F32R)
        rf = [sbuf(layers, f"rf{i}", [P, T]) for i in range(4)]
        hs = [sbuf(layers, f"hs{u}", [P, T]) for u in range(2)]
        shi = [sbuf(layers, f"shi{u}", [P, T], F32R) for u in range(2)]
        slo = [sbuf(layers, f"slo{u}", [P, T], F32R) for u in range(2)]
        layers.close()

        rows = sbuf(pre, "rows", [TT, NTILE, ROW])
        xf = [sbuf(pre, f"xf{u}", [P, KD, T]) for u in range(2)]
        lgT = [sbuf(pre, f"lgT{u}", [E, T]) for u in range(2)]
        lg = sbuf(pre, "lg", [TT, NTILE, E])
        r8 = [sbuf(pre, f"r8{i}", [TT, NTILE, E]) for i in range(3)]
        m16 = sbuf(pre, "m16", [TT, NTILE, 2 * E], BF16)
        p16 = sbuf(pre, "p16", [TT, NTILE, 2 * E])
        k16 = sbuf(pre, "k16", [TT, NTILE, 2 * E])
        q16 = sbuf(pre, "q16", [TT, NTILE, 2 * E])
        cnt = sbuf(pre, "cnt", [TT, G, E])
        r1 = [sbuf(pre, f"r1{i}", [TT, NTILE]) for i in range(3)]
        top = sbuf(pre, "top", [TT, NTILE, 2])
        t2 = [sbuf(pre, f"t2{i}", [TT, NTILE, 2]) for i in range(4)]
        slot = sbuf(pre, "slot", [TT, NTILE, 2], U32)
        pre.close()

        whi = sbuf(ctx, "whi", [P, 2 * KD, H], F32R)
        wlo = sbuf(ctx, "wlo", [P, 2 * KD, H], F32R)
        wohi = sbuf(ctx, "wohi", [P, NH, D], F32R)
        wolo = sbuf(ctx, "wolo", [P, NH, D], F32R)
        gxhi = [sbuf(ctx, f"gxhi{j}", [P, KD, NC], F32R) for j in range(NJ)]
        gxlo = [sbuf(ctx, f"gxlo{j}", [P, KD, NC], F32R) for j in range(NJ)]
        gr = [sbuf(ctx, f"gr{j}", [SMAX, ST, ROW]) for j in range(NJ)]
        gate = [sbuf(ctx, f"gate{j}", [SMAX, ST]) for j in range(NJ)]
        tix = [sbuf(ctx, f"tix{j}", [SMAX, ST], U32) for j in range(NJ)]
        gl = [sbuf(ctx, f"gl{i}", [P, NC]) for i in range(2)]
        hm = [sbuf(ctx, f"hm{i}", [P, NC]) for i in range(2)]
        mhi = sbuf(ctx, "mhi", [P, NH, NC], F32R)
        mlo = sbuf(ctx, "mlo", [P, NH, NC], F32R)
        ys = [sbuf(ctx, f"ys{i}", [SMAX, D]) for i in range(ST)]

        def psum(name):
            return ctx.enter_context(nc.psum_tensor(name, [P, 1024], F32))

        X, O, S, R = psum("X"), psum("O"), psum("S"), psum("R")

        def banks(t, n, m=P):
            return t[0:m, :].rearrange("p (k n) -> p k n", k=2)[:, :, 0:n]

        def tok3(t):
            return t[0:TT, 0:TPC * D].rearrange("p (t n) -> p t n", t=TPC)

        quarter = [S[:, 0:512], S[:, 512:1024], R[:, 0:512], R[:, 512:1024]]

        names = """first_loaded loaded patch0 patch1 txt0 txt1 set_hi set_gam set_dve set_act set_pe set_pool zero_ready quant passed
        wp_hi wp_lo ehi_done elo_done e_ps e_emb e_txt e_tr e_h
        bn_done mv_done ve_done rstd_done xn_done xT_done hi_done lo_done
        k_ps q_ps v_ps zk_done zq_done rot_k rot_q kR_done qR_done v_done w_ps wm_done wa_done we_done wl_done
        wp_done ao_ps ao_sb a_tr a_res
        f_ps f_relu f_hi f_split fo_ps fo_sb f_tr f_res
        s_ps s_scan s_hi s_lo so_ps so_sb s_tr s_res
        h_out rx_done lgt_ps lgt_sb lg_ps lg_sb rt rt_act rt_pe scattered xz_done
        w_load wo_load w_hi w_lo wo_hi wo_lo row0 row1 row2 gx_ps gx_hi gx_lo meta
        up_ps gl_done hm_done mhi_done mlo_done y_ps y_sb added settled""".split()
        s = {n: sem(n) for n in names}
        patch_loaded, txt_loaded, row_loaded = [s["patch0"], s["patch1"]], [s["txt0"], s["txt1"]], [s["row0"], s["row1"], s["row2"]]

        block = ctx.enter_context(nc.Block())

        def stand_alone(e):
            e.sem_inc(s["passed"], 1)

        def chunks(e, body, n):
            body(0, 0, True, False)
            body(1, 1, False, False)
            with e.Fori(1, n // 2 - 1) as i:
                body(i * 2, 0, False, False)
                body(i * 2 + 1, 1, False, False)
            body(n - 2, 0, False, False)
            body(n - 1, 1, False, True)

        def tiles(a, c, n=TPC):
            return a[:, c * n:(c + 1) * n, :] if fixed(c) else a[:, bass.ds(c * n, n), :]

        N_FIRST, N_LOADED = 6, 24

        wflat = wst[:].rearrange("p a n -> p (a n)")
        oflat = wost[:].rearrange("p a n -> p (a n)")

        def wst_view(n, at_, k):
            return wst[:].rearrange("p a n -> p (a n)")[:, at_:at_ + n].rearrange("p (k n) -> p k n", k=k)

        wp_st = wst_view(KP * D, 0, KP)
        k_st, q_st, v_st, p_st = (wst_view(KD * D, KP * D + i * KD * D, KD) for i in range(4))
        c_st = wflat[:, 3584:3584 + D]
        b_st = wst_view(KD * NS, 3840, KD)
        w2_st = oflat[:, 0:KF * D].rearrange("p (k n) -> p k n", k=KF)
        zrow = wflat[:, 4096:4096 + ROW]
        tst = [wflat[:, 4400 + u * 512:4912 + u * 512].rearrange("p (k b n) -> p k b n", k=KD, b=GSEQ) for u in range(2)]

        before = [t[0:TT, 0:NTILE * E].rearrange("p (t e) -> p t e", e=2 * E) for t in (O, S)]
        RT_CHOICES, RT_ALL = 16, 32

        def pair8(a):
            return a[:].rearrange("p t (c e) -> p t c e", c=2)

        def load_expert(sp, e):
            one = bass.ds(e, 1)
            for i, w in enumerate((w0, w1)):
                sp.dma_start(wst[:, i * KD:(i + 1) * KD, :],
                             w[one].rearrange("e (k p) h -> (e p) k h", p=P)).then_inc(s["w_load"], 16)
            full = NH - 1
            sp.dma_start(wost[:, 0:full, :],
                         wo[one, 0:full * P, :].rearrange("e (t p) n -> (e p) t n", p=P)).then_inc(s["wo_load"], 16)
            sp.dma_start(wost[0:HT[-1][1], full, :],
                         wo[one, full * P:H, :].rearrange("e p n -> (e p) n")).then_inc(s["wo_load"], 16)

        def load_rows(sp, e, j):
            c0, n = CHUNKS[j]
            a, last = slot_tiles(n)[0][1], slot_tiles(n)[2][1]
            ex = xrows.rearrange("(e r) n -> e r n", e=E)[bass.ds(e, 1)]
            sp.dma_start(gr[j][0:a, 0:2, :],
                         ex[:, c0:c0 + 2 * a, :].rearrange("e (t p) n -> (e p) t n", p=a)).then_inc(row_loaded[j], 16)
            sp.dma_start(gr[j][0:last, 2, :],
                         ex[:, c0 + 2 * a:c0 + n, :].rearrange("e p n -> (e p) n")).then_inc(row_loaded[j], 16)

        @block.sync
        def _(sp):
            for dst, src in ((idt[:], ident), (wst_view(1536, 0, KP), w_patch), (clst[:], cls), (pos0t[:], pos0),
                             (posb[:], pos), (tokbt[:], tok_b)):
                sp.dma_start(dst, src).then_inc(s["first_loaded"], 16)
            for g in range(2):
                sp.dma_start(pst[g][:], patches[g]).then_inc(patch_loaded[g], 16)
                sp.dma_start(tst[g], txt[g]).then_inc(txt_loaded[g], 16)
            for dst, src in (
                (k_st, w_k), (q_st, w_q), (v_st, w_vT), (p_st, w_p), (b_st, b_wT), (c_st, c_wT),
                (w1st[:], w1T), (w2_st, w2T), (bkt[:], b_k), (bqt[:], b_q), (bvt[:], b_v), (bpt[:], b_p),
                (b1t[:], b1), (b2t[:], b2), (lat[:], log_a), (dpt[:], d_param), (cosT[:], rot_cos),
                (sinT[:], rot_sin), (msk[:], mask), (wr[:], w_r), (base[:], slotbase),
            ):
                sp.dma_start(dst, src).then_inc(s["loaded"], 16)
            sp.dma_start(rev[:], revno).then_inc(s["loaded"], 16)
            sp.dma_start(upf[:], upper).then_inc(s["loaded"], 16)
            sp.dma_start(tno[:], tokno).then_inc(s["loaded"], 16)
            with sp.Fori(1, G // 2) as i:
                for u in range(2):
                    one = bass.ds(i * 2 + u, 1)
                    sp.wait_ge(s["elo_done"], i * 2 + (u - 1))
                    sp.dma_start(pst[u][:], patches[one].rearrange("a p b n -> (a p) b n")).then_inc(patch_loaded[u], 16)
                    sp.wait_ge(s["e_txt"], i * 2 + (u - 1))
                    sp.dma_start(tst[u], txt[one].rearrange("a p k b n -> (a p) k b n")).then_inc(txt_loaded[u], 16)
            sp.wait_ge(s["zero_ready"], 2)
            sp.dma_start(xrows.rearrange("(p a) n -> p a n", p=P),
                         zrow.unsqueeze(1).to_broadcast([P, NROW // P, ROW])).then_inc(s["xz_done"], 16)
            sp.wait_ge(s["xz_done"], 16)
            sp.wait_ge(s["set_dve"], 3)
            load_expert(sp, 0)
            sp.wait_ge(s["s_res"], NCH)
            sp.dma_start(out.rearrange("(t p) n -> p t n", p=TT), h[:]).then_inc(s["h_out"], 16)
            sp.wait_ge(s["scattered"], 16 * 2 * NTILE)
            sp.wait_ge(s["h_out"], 16)
            for j in range(NJ):
                load_rows(sp, 0, j)
            with sp.Fori(0, E - 1) as e:
                sp.wait_ge(s["w_lo"], e * NH + NH)
                sp.wait_ge(s["wo_lo"], e * NH + NH)
                load_expert(sp, e + 1)
                for j in range(NJ):
                    sp.wait_ge(s["gx_ps"], e * NJ + j + 1)
                    sp.wait_ge(s["meta"], e * NJ + j + 1)
                    load_rows(sp, e + 1, j)
            sp.wait_ge(s["h_out"], 16)
            sp.wait_ge(s["added"], 16 * ST * NJ * E)

        def ln_stats(dve, n, c):
            for t in range(TPC):
                i = nc.vector.bn_stats(st[:, t, :], tiles(h, c)[:, t, :])
            i.then_inc(s["bn_done"], 1)
            dve.wait_ge(s["bn_done"], n + 1)
            stand_alone(dve)
            for t in range(TPC):
                i = nc.vector.bn_aggr(mv[:, t, :], st[:, t, :])
            i.then_inc(s["mv_done"], 1)

        def ln_rstd(pool, n):
            pool.wait_ge(s["mv_done"], n + 1)
            nc.gpsimd.tensor_tensor(ve[:], mv[:, :, 1], epst[:], ALU.add).then_inc(s["ve_done"], 1)
            pool.wait_ge(s["ve_done"], n + 1)
            nc.gpsimd.tensor_tensor(rstd[:], ve[:], mhalf[:], ALU.pow).then_inc(s["rstd_done"], 1)

        def ln_norm(dve, n, c):
            dve.wait_ge(s["rstd_done"], n + 1)
            if not (fixed(n) and n == 0):
                dve.wait_ge(s["xT_done"], n)
            for t in range(TPC):
                i = nc.vector.tensor_scalar(xt[:, t, :], tiles(h, c)[:, t, :], mv[:, t, 0:1], rstd[:, t:t + 1],
                                            ALU.subtract, ALU.mult)
            i.then_inc(s["xn_done"], 1)

        def ln_transpose(pe, n):
            pe.wait_ge(s["xn_done"], n + 1)
            for t in range(TPC):
                for k in range(KD):
                    i = nc.tensor.transpose(banks(X, T)[:, k, t * TT:(t + 1) * TT], xt[:, t, k * P:(k + 1) * P],
                                            idt[0:TT, 0:TT])
            i.then_inc(s["xT_done"], 1)

        def ln_hi(act, n, u):
            act.wait_ge(s["xT_done"], n + 1)
            nc.scalar.activation(xhi[u][:], banks(X, T), ACT.Copy).then_inc(s["hi_done"], 1)

        def ln_lo(dve, n, u):
            dve.wait_ge(s["hi_done"], n + 1)
            nc.vector.tensor_tensor(xlo[u][:], banks(X, T), xhi[u][:].bitcast(F32), ALU.subtract).then_inc(s["lo_done"], 1)

        def add_back(dve, c, transposed, added):
            dve.wait_ge(transposed, c + 1)
            nc.vector.tensor_tensor(tiles(h, c), tiles(h, c), tok3(X), ALU.add).then_inc(added, 1)

        def back_transpose(done):
            for t in range(TPC):
                for k in range(KD):
                    i = nc.tensor.transpose(tok3(X)[:, t, k * P:(k + 1) * P], oT[:, k, t * TT:(t + 1) * TT], idt[:])
            i.then_inc(done, 1)

        def mm3(o, ahi, alo, xh, xl, start, stop):
            nc.tensor.matmul(o, ahi, xh, start=start, stop=False)
            nc.tensor.matmul(o, ahi, xl, start=False, stop=False)
            return nc.tensor.matmul(o, alo, xh, start=False, stop=stop)

        @block.tensor
        def _(pe):
            pe.wait_ge(s["wp_lo"], 1)
            pe.wait_ge(s["first_loaded"], 16 * N_FIRST)

            def embed_back(g, u, gfirst):
                pe.wait_ge(s["e_emb"], g + 1)
                pe.wait_ge(s["e_txt"], g + 1)
                for c, dst in enumerate((X, O)):
                    if not gfirst:
                        pe.wait_ge(s["e_h"], g * 2 + c - 1)
                    for t in range(TPC):
                        for k in range(KD):
                            em = emb[u][:, k].rearrange("p b l -> p (b l)")
                            i = nc.tensor.transpose(tok3(dst)[:, t, k * P:(k + 1) * P],
                                                    em[:, c * T + t * TT:c * T + (t + 1) * TT], idt[:])
                    i.then_inc(s["e_tr"], 1)

            def embed(g, u, first, last):
                pe.wait_ge(s["elo_done"], g + 1)
                if not (fixed(g) and g < 2):
                    pe.wait_ge(s["e_emb"], g - 1)
                for m in range(KD):
                    for k in range(KP):
                        i = mm3(banks((S, R)[u], GP)[:, m, :], wphi[:, k, m * P:(m + 1) * P],
                                wplo[:, k, m * P:(m + 1) * P], ehi[u][:, k, :], elo[u][:, k, :], k == 0, k == KP - 1)
                i.then_inc(s["e_ps"], 1)
                if not first:
                    embed_back(g - 1, 1 - u, fixed(g) and g == 1)
                if last:
                    embed_back(g, u, False)

            chunks(pe, embed, G)
            pe.wait_ge(s["loaded"], 16 * N_LOADED)
            pe.wait_ge(s["set_dve"], 1)
            for m in range(KD):
                for k in range(KD):
                    nc.tensor.matmul(S[:, m * 512:m * 512 + D], v_st[:, k, m * P:(m + 1) * P], p_st[:, k, :],
                                     start=k == 0, stop=k == KD - 1)
            for k in range(KD):
                i = nc.tensor.matmul(R[0:L, 0:D], bvx[:, k, :], p_st[:, k, :], start=k == 0, stop=k == KD - 1)
            i.then_inc(s["set_pe"], 1)
            pe.wait_ge(s["set_gam"], 2)
            nc.tensor.matmul(R[:, 512:514], onesf[:], gsum[:], start=True, stop=True).then_inc(s["set_pe"], 1)

            pe.wait_ge(s["set_dve"], 3)
            pe.wait_ge(s["set_act"], 1)
            pe.wait_ge(s["e_h"], 2 * G)
            ln_transpose(pe, 0)

            def weighted_sum(c, u, cfirst):
                pe.wait_ge(s["wp_done"], c + 1)
                if not cfirst:
                    pe.wait_ge(s["ao_sb"], c)
                for b in range(SEQ):
                    for m in range(KD):
                        i = nc.tensor.matmul(banks(O, T)[:, m, b * L:(b + 1) * L], vp[u][:, b, m * P:(m + 1) * P],
                                             wp[u][:, b * L:(b + 1) * L], start=True, stop=True)
                i.then_inc(s["ao_ps"], 1)

            def attention(c, u, first, last):
                pe.wait_ge(s["lo_done"], c + 1)
                if not first:
                    pe.wait_ge(s["v_done"], c)
                for dst, hi, lo, done in ((S, khi, klo, s["k_ps"]), (R, qhi, qlo, s["q_ps"])):
                    if dst is R and not first:
                        pe.wait_ge(s["wm_done"], c)
                    for m in range(KD):
                        for k in range(KD):
                            i = mm3(banks(dst, T)[:, m, :], hi[:, k, m * P:(m + 1) * P], lo[:, k, m * P:(m + 1) * P],
                                    xhi[u][:, k, :], xlo[u][:, k, :], k == 0, k == KD - 1)
                    i.then_inc(done, 1)
                pe.wait_ge(s["zk_done"], c + 1)
                for b in range(SEQ):
                    for k in range(KD):
                        xs = slice(b * L, (b + 1) * L)
                        o = S[0:L, b * D:(b + 1) * D]
                        nc.tensor.matmul(o, xhi[u][:, k, xs], vhi[:, k, :], start=k == 0, stop=False)
                        nc.tensor.matmul(o, xhi[u][:, k, xs], vlo[:, k, :], start=False, stop=False)
                        i = nc.tensor.matmul(o, xlo[u][:, k, xs], vhi[:, k, :], start=False, stop=k == KD - 1)
                i.then_inc(s["v_ps"], 1)
                if not first:
                    weighted_sum(c - 1, 1 - u, fixed(c) and c == 1)
                    pe.wait_ge(s["ao_sb"], c)
                    back_transpose(s["a_tr"])
                pe.wait_ge(s["qR_done"], c + 1)
                for b in range(SEQ):
                    bs = slice(b * L, (b + 1) * L)
                    for k in range(KD):
                        i = nc.tensor.matmul(R[0:L, bs], qR[:, k, bs], kR[:, k, bs], start=k == 0, stop=k == KD - 1)
                i.then_inc(s["w_ps"], 1)
                if not first:
                    pe.wait_ge(s["a_res"], c)
                if not last:
                    ln_transpose(pe, c + 1)
                else:
                    weighted_sum(c, u, False)
                    pe.wait_ge(s["ao_sb"], c + 1)
                    back_transpose(s["a_tr"])
                    pe.wait_ge(s["a_res"], NCH)
                    ln_transpose(pe, NCH)

            chunks(pe, attention, NCH)

            def ffn(c, u, first, last):
                n = c + NCH
                pe.wait_ge(s["lo_done"], n + 1)
                for f in range(KF):
                    if f >= 4 or not first:
                        pe.wait_ge(s["f_relu"], c * KF + f - 3)
                    o = quarter[f % 4][:, 0:T]
                    for k in range(KD):
                        w = w1q[:, k, f * P:(f + 1) * P]
                        nc.tensor.matmul(o, w, xhi[u][:, k, :], start=k == 0, stop=False)
                        i = nc.tensor.matmul(o, w, xlo[u][:, k, :], start=False, stop=k == KD - 1)
                    i.then_inc(s["f_ps"], 1)
                    if f == 3 and not first:
                        pe.wait_ge(s["fo_sb"], c)
                        back_transpose(s["f_tr"])
                if not last:
                    if not first:
                        pe.wait_ge(s["f_res"], c)
                    ln_transpose(pe, n + 1)
                for f in range(KF):
                    pe.wait_ge(s["f_split"], c * KF + f + 1)
                    for m in range(KD):
                        w = w2q[:, f, m * P:(m + 1) * P]
                        nc.tensor.matmul(banks(O, T)[:, m, :], w, hhi[:, f, :], start=f == 0, stop=False)
                        i = nc.tensor.matmul(banks(O, T)[:, m, :], w, hlo[:, f, :], start=False, stop=f == KF - 1)
                i.then_inc(s["fo_ps"], 1)
                if last:
                    pe.wait_ge(s["fo_sb"], c + 1)
                    pe.wait_ge(s["f_res"], c)
                    back_transpose(s["f_tr"])
                    pe.wait_ge(s["f_res"], NCH)
                    ln_transpose(pe, 2 * NCH)

            chunks(pe, ffn, NCH)

            def ssm_out(c, u, cfirst):
                pe.wait_ge(s["s_lo"], c + 1)
                if not cfirst:
                    pe.wait_ge(s["so_sb"], c)
                for m in range(KD):
                    ms = slice(m * P, (m + 1) * P)
                    o = banks(O, T)[:, m, :]
                    mm3(o, chi[:, ms], clo[:, ms], shi[u][:], slo[u][:], True, False)
                    i = mm3(o, dhi[:, m, :], dlo[:, m, :], xhi[u][:, m, :], xlo[u][:, m, :], False, True)
                i.then_inc(s["so_ps"], 1)

            def ssm(c, u, first, last):
                n = c + 2 * NCH
                early = fixed(c) and c < 2
                pe.wait_ge(s["lo_done"], n + 1)
                if not early:
                    pe.wait_ge(s["s_scan"], c - 1)
                for k in range(KD):
                    i = mm3(quarter[u][:, 0:T], bhi[:, k, :], blo[:, k, :], xhi[u][:, k, :], xlo[u][:, k, :],
                            k == 0, k == KD - 1)
                i.then_inc(s["s_ps"], 1)
                if not early:
                    pe.wait_ge(s["so_sb"], c - 1)
                    back_transpose(s["s_tr"])
                if not first:
                    ssm_out(c - 1, 1 - u, fixed(c) and c == 1)
                if not early:
                    pe.wait_ge(s["s_res"], c - 1)
                if not last:
                    ln_transpose(pe, n + 1)
                else:
                    pe.wait_ge(s["so_sb"], c)
                    back_transpose(s["s_tr"])
                    ssm_out(c, u, False)
                    pe.wait_ge(s["s_res"], c)
                    pe.wait_ge(s["so_sb"], c + 1)
                    back_transpose(s["s_tr"])

            chunks(pe, ssm, NCH)

            pe.wait_ge(s["s_res"], NCH)

            def logits(c, u):
                pe.wait_ge(s["rx_done"], c + 1)
                for k in range(KD):
                    i = nc.tensor.matmul(quarter[u][0:E, 0:T], wr[:, k, :], xf[u][:, k, :],
                                         start=k == 0, stop=k == KD - 1)
                i.then_inc(s["lgt_ps"], 1)
                pe.wait_ge(s["lgt_sb"], c + 1)
                if not (fixed(c) and c < 2):
                    pe.wait_ge(s["lg_sb"], c - 1)
                stand_alone(pe)
                for t in range(TPC):
                    o = R[0:TT, u * 512 + t * E:u * 512 + (t + 1) * E]
                    i = nc.tensor.transpose(o, lgT[u][:, t * TT:(t + 1) * TT], idt[0:E, 0:E])
                i.then_inc(s["lg_ps"], 1)

            def router(c, u, first, last):
                if not first:
                    pe.wait_ge(s["rx_done"], c)
                ln_transpose(pe, c + 3 * NCH)
                if not first:
                    logits(c - 1, 1 - u)
                if last:
                    logits(c, u)

            chunks(pe, router, NCH)
            pe.wait_ge(s["rt"], RT_CHOICES)
            for g in range(G):
                mg = m16[:, g * TPG:(g + 1) * TPG, :]
                gb = before[g // 4][:, (g % 4) * TPG:(g % 4 + 1) * TPG, :]
                nc.tensor.matmul(gb, up[:], mg, start=True, stop=False)
                for t in range(TPG - 1):
                    n = TPG - 1 - t
                    nc.tensor.matmul(gb[:, t + 1:, :], ones[:], mg[:, t:t + 1, :].to_broadcast([TT, n, 2 * E]),
                                     start=False, stop=t == TPG - 2)
                for t in range(TPG):
                    i = nc.tensor.matmul(X[0:TT, g * E:(g + 1) * E], ones[:], mg[:, t, 0:E],
                                         start=t == 0, stop=t == TPG - 1)
            i.then_inc(s["rt_pe"], 1)

            def gx_transpose(e, j, first):
                pe.wait_ge(row_loaded[j], e * 32 + 32)
                if not first:
                    pe.wait_ge(s["gx_lo"], e * NJ + j)
                n = CHUNKS[j][1]
                for t, (a0, a) in enumerate(slot_tiles(n)):
                    for k in range(KD):
                        i = nc.tensor.transpose(banks(X, n)[:, k, a0:a0 + a], gr[j][0:a, t, k * P:(k + 1) * P],
                                                idt[0:a, 0:a])
                i.then_inc(s["gx_ps"], 1)

            pe.wait_ge(s["rt"], RT_ALL)
            pe.sem_inc(s["y_ps"], 1)
            gx_transpose(0, 0, True)

            def expert(e, last):
                for j, (_, n) in enumerate(CHUNKS):
                    q = e * NJ + j
                    pe.wait_ge(s["gx_lo"], q + 1)
                    for i, (h0, hn) in enumerate(HT):
                        if j == 0:
                            pe.wait_ge(s["w_lo"], e * NH + i + 1)
                        pe.wait_ge(s["hm_done"], q * NH + (NH + i - 1 if i else NH))
                        for w in range(2):
                            for k in range(KD):
                                ins = mm3(banks((S, R)[i % 2], n, hn)[:, w, :], whi[:, w * KD + k, h0:h0 + hn],
                                          wlo[:, w * KD + k, h0:h0 + hn], gxhi[j][:, k, 0:n], gxlo[j][:, k, 0:n],
                                          k == 0, k == KD - 1)
                        ins.then_inc(s["up_ps"], 1)
                    if j < NJ - 1:
                        gx_transpose(e, j + 1, False)
                    elif not last:
                        gx_transpose(e + 1, 0, False)
                    for t, (a0, a) in enumerate(slot_tiles(n)):
                        pe.wait_ge(s["y_sb"], q * ST + (ST, ST - 1, ST + 1)[t])
                        o = O[0:a, (t % 2) * 512:(t % 2) * 512 + D]
                        for i, (h0, hn) in enumerate(HT):
                            if t == 0:
                                pe.wait_ge(s["mlo_done"], q * NH + i + 2)
                                if j == 0:
                                    pe.wait_ge(s["wo_lo"], e * NH + i + 1)
                            lh, ll = mhi[0:hn, i, a0:a0 + a], mlo[0:hn, i, a0:a0 + a]
                            nc.tensor.matmul(o, lh, wohi[0:hn, i, :], start=i == 0, stop=False)
                            nc.tensor.matmul(o, lh, wolo[0:hn, i, :], start=False, stop=False)
                            ins = nc.tensor.matmul(o, ll, wohi[0:hn, i, :], start=False, stop=i == NH - 1)
                        ins.then_inc(s["y_ps"], 1)

            with pe.Fori(0, E - 1) as e:
                expert(e, False)
            expert(E - 1, True)

        @block.scalar
        def _(act):
            act.preload_act_table_set("natural_log_exp_and_others")
            act.wait_ge(s["first_loaded"], 16 * N_FIRST)
            nc.scalar.activation(wphi[:], wp_st, ACT.Copy).then_inc(s["wp_hi"], 1)

            def embed_out(g):
                for c, src in enumerate((X, O)):
                    act.wait_ge(s["e_tr"], g * 2 + c + 1)
                    nc.scalar.activation(tiles(h, g * 2 + c), tok3(src), ACT.Copy).then_inc(s["e_h"], 1)

            def embed(g, u, first, last):
                act.wait_ge(patch_loaded[u], (g - u) * 8 + 16 if not fixed(g) else 16 * (g // 2 + 1))
                if not (fixed(g) and g < 2):
                    act.wait_ge(s["e_ps"], g - 1)
                nc.scalar.activation(ehi[u][:], pst[u][:], ACT.Copy).then_inc(s["ehi_done"], 1)
                if not (fixed(g) and g < 2):
                    embed_out(g - 2)
                if last:
                    embed_out(g - 1)
                    embed_out(g)

            chunks(act, embed, G)
            act.wait_ge(s["loaded"], 16 * N_LOADED)
            act.wait_ge(s["set_dve"], 1)
            nc.scalar.activation(w1q[:], w1st[:], ACT.Abs, accum_out=gsum[:, 0:1]).then_inc(s["set_gam"], 1)
            nc.scalar.activation(w2q[:], w2_st, ACT.Abs, accum_out=gsum[:, 1:2]).then_inc(s["set_gam"], 1)
            for dst, src in ((khi, k_st), (qhi, q_st), (bhi, b_st), (dhi, dmat[:])):
                nc.scalar.activation(dst[:], src, ACT.Copy)
            nc.scalar.activation(chi[:], c_st, ACT.Copy)
            act.wait_ge(s["set_pe"], 1)
            nc.scalar.activation(vhi[:], banks(S, D), ACT.Copy)
            nc.scalar.activation(bvp[:], R[0:L, 0:D], ACT.Copy).then_inc(s["set_hi"], 1)
            nc.scalar.activation(at[:], lat[:].to_broadcast([P, L]), ACT.Exp).then_inc(s["set_act"], 1)

            ln_hi(act, 0, 0)

            def result(c, src_done, out_done, tr_done, bias, cfirst):
                act.wait_ge(src_done, c + 1)
                if not cfirst:
                    act.wait_ge(tr_done, c)
                if bias is None:
                    i = nc.scalar.activation(oT[:], banks(O, T), ACT.Copy)
                else:
                    for m in range(KD):
                        i = nc.scalar.activation(oT[:, m, :], banks(O, T)[:, m, :], ACT.Identity, bias=bias[:, m:m + 1])
                i.then_inc(out_done, 1)

            def attention(c, u, first, last):
                for z, src, bias, ps_done, z_done, rot in (
                        (zk, S, bkt, s["k_ps"], s["zk_done"], s["kR_done"]), (zq, R, bqt, s["q_ps"], s["zq_done"], s["qR_done"])):
                    act.wait_ge(ps_done, c + 1)
                    if not first:
                        act.wait_ge(rot, c)
                    for m in range(KD):
                        i = nc.scalar.activation(z[:, m, :], banks(src, T)[:, m, :], ACT.Identity, bias=bias[:, m:m + 1])
                    i.then_inc(z_done, 1)
                if not first:
                    result(c - 1, s["ao_ps"], s["ao_sb"], s["a_tr"], bpt, fixed(c) and c == 1)
                act.wait_ge(s["wm_done"], c + 1)
                if not first:
                    act.wait_ge(s["wp_done"], c)
                nc.scalar.activation(wa[:], wm[:], ACT.Abs).then_inc(s["wa_done"], 1)
                act.wait_ge(s["wa_done"], c + 1)
                nc.scalar.activation(we[:], wa[:], ACT.Exp, scale=-1.0).then_inc(s["we_done"], 1)
                act.wait_ge(s["we_done"], c + 1)
                nc.scalar.activation(wl[:], we[:], ACT.Ln, bias=1.0).then_inc(s["wl_done"], 1)
                if last:
                    result(c, s["ao_ps"], s["ao_sb"], s["a_tr"], bpt, False)
                ln_hi(act, c + 1, 1 - u)

            chunks(act, attention, NCH)

            def ffn(c, u, first, last):
                n = c + NCH
                for f in range(KF):
                    act.wait_ge(s["f_ps"], c * KF + f + 1)
                    if f >= 4 or not first:
                        act.wait_ge(s["f_split"], c * KF + f - 3)
                    nc.scalar.activation(rf[f % 4][:], quarter[f % 4][:, 0:T], ACT.Relu, bias=b1t[:, f:f + 1])
                    if f == 0 and not first:
                        act.wait_ge(s["fo_ps"], c)
                    nc.scalar.activation(hhi[:, f, :], quarter[f % 4][:, 0:T], ACT.Relu,
                                         bias=b1t[:, f:f + 1]).then_inc(s["f_relu"], 1)
                    if f == 0 and not first:
                        result(c - 1, s["fo_ps"], s["fo_sb"], s["f_tr"], b2t, fixed(c) and c == 1)
                if last:
                    result(c, s["fo_ps"], s["fo_sb"], s["f_tr"], b2t, False)
                ln_hi(act, n + 1, 1 - u)

            chunks(act, ffn, NCH)

            def ssm(c, u, first, last):
                n = c + 2 * NCH
                early = fixed(c) and c < 2
                if not first:
                    result(c - 1, s["so_ps"], s["so_sb"], s["s_tr"], None, fixed(c) and c == 1)
                act.wait_ge(s["s_scan"], c + 1)
                if not early:
                    act.wait_ge(s["so_ps"], c - 1)
                nc.scalar.activation(shi[u][:], hs[u][:], ACT.Copy).then_inc(s["s_hi"], 1)
                if not last:
                    ln_hi(act, n + 1, 1 - u)
                else:
                    result(c, s["so_ps"], s["so_sb"], s["s_tr"], None, False)

            chunks(act, ssm, NCH)

            def router(c, u, first, last):
                def logits_out(c, u):
                    act.wait_ge(s["lgt_ps"], c + 1)
                    if not (fixed(c) and c < 2):
                        act.wait_ge(s["lg_ps"], c - 1)
                    nc.scalar.activation(lgT[u][:], quarter[u][0:E, 0:T], ACT.Copy).then_inc(s["lgt_sb"], 1)
                    act.wait_ge(s["lg_ps"], c + 1)
                    nc.scalar.activation(tiles(lg, c), R[0:TT, u * 512:u * 512 + TPC * E].rearrange(
                        "p (t e) -> p t e", t=TPC), ACT.Copy).then_inc(s["lg_sb"], 1)

                act.wait_ge(s["xT_done"], c + 3 * NCH + 1)
                if not (fixed(c) and c < 2):
                    act.wait_ge(s["lgt_ps"], c - 1)
                nc.scalar.activation(xf[u][:], banks(X, T), ACT.Copy).then_inc(s["rx_done"], 1)
                if not first:
                    logits_out(c - 1, 1 - u)
                if last:
                    logits_out(c, u)

            chunks(act, router, NCH)
            act.wait_ge(s["rt"], 2)
            nc.scalar.activation(r8[1][:], r8[0][:], ACT.Exp).then_inc(s["rt_act"], 1)

            def split_w(e, i, a=0):
                h0, hn = HT[i]
                nc.scalar.activation(whi[:, :, h0:h0 + hn], wst[:, :, h0:h0 + hn], ACT.Copy).then_inc(s["w_hi"], 1)

            act.wait_ge(s["scattered"], 16 * 2 * NTILE)
            act.wait_ge(s["h_out"], 16)
            act.wait_ge(s["rt"], RT_ALL)
            act.sem_inc(s["y_sb"], ST)
            act.wait_ge(s["w_load"], 32)
            for i in range(NH):
                split_w(0, i)
            act.wait_ge(s["gx_ps"], 1)
            nc.scalar.activation(gxhi[0][:, :, 0:CHUNKS[0][1]], banks(X, CHUNKS[0][1]), ACT.Copy).then_inc(s["gx_hi"], 1)

            def expert(e, last):
                for j, (_, n) in enumerate(CHUNKS):
                    q = e * NJ + j

                    def hidden_hi(i):
                        hn = HT[i][1]
                        act.wait_ge(s["hm_done"], q * NH + i + 1 + NH)
                        nc.scalar.activation(mhi[0:hn, i, 0:n], hm[i % 2][0:hn, 0:n], ACT.Copy).then_inc(s["mhi_done"], 1)

                    if j == 0:
                        act.wait_ge(s["wo_load"], e * 32 + 32)
                    if j == NJ - 1 and not last:
                        act.wait_ge(s["w_load"], e * 32 + 64)
                    for i, (h0, hn) in enumerate(HT):
                        act.wait_ge(s["up_ps"], q * NH + i + 1)
                        act.wait_ge(s["hm_done"], q * NH + i - 1 + NH)
                        nc.scalar.activation(gl[i % 2][0:hn, 0:n], banks((S, R)[i % 2], n, hn)[:, 0, :],
                                             ACT.Gelu_apprx_tanh).then_inc(s["gl_done"], 1)
                        if i == 0:
                            act.wait_ge(s["y_ps"], q * ST + 1)
                        if i:
                            hidden_hi(i - 1)
                        if j == 0:
                            nc.scalar.activation(wohi[0:hn, i, :], wost[0:hn, i, :], ACT.Copy).then_inc(s["wo_hi"], 1)
                        if j == NJ - 1 and not last:
                            split_w(e + 1, i)
                    hidden_hi(NH - 1)
                    if not (last and j == NJ - 1):
                        nn = CHUNKS[(j + 1) % NJ][1]
                        act.wait_ge(s["gx_ps"], q + 2)
                        nc.scalar.activation(gxhi[(j + 1) % NJ][:, :, 0:nn], banks(X, nn), ACT.Copy).then_inc(s["gx_hi"], 1)
                    for t, (a0, a) in enumerate(slot_tiles(n)):
                        act.wait_ge(s["y_ps"], q * ST + t + 2)
                        act.wait_ge(s["meta"], q + 1)
                        act.wait_ge(s["settled"], q * ST + t - ST + 1 + ST * NJ)
                        nc.scalar.activation(ys[t][0:a, :], O[0:a, (t % 2) * 512:(t % 2) * 512 + D], ACT.Copy,
                                             scale=gate[j][0:a, t:t + 1]).then_inc(s["y_sb"], 1)

            with act.Fori(0, E - 1) as e:
                expert(e, False)
            expert(E - 1, True)

        @block.vector
        def _(dve):
            nc.vector.memset(mhalf[:], -0.5).then_inc(s["set_pool"], 1)
            nc.vector.memset(epst[:], EPS).then_inc(s["set_pool"], 1)
            nc.vector.memset(onesf[:], 1.0).then_inc(s["set_pool"], 1)
            nc.vector.memset(ones[:], 1.0).then_inc(s["set_pool"], 1)
            dve.wait_ge(s["first_loaded"], 16 * N_FIRST)
            nc.vector.tensor_tensor(clst[:], clst[:], pos0t[:], ALU.add).then_inc(s["quant"], 1)
            nc.vector.tensor_tensor(posb[:], posb[:], tokbt[:].unsqueeze(2).to_broadcast([P, KD, NPATCH]),
                                    ALU.add).then_inc(s["quant"], 1)
            dve.wait_ge(s["quant"], 2)
            for u in range(2):
                for k in range(KD):
                    nc.vector.tensor_copy(emb[u][:, k, :, 0], clst[:, k:k + 1].to_broadcast([P, GSEQ]))
            dve.wait_ge(s["wp_hi"], 1)
            nc.vector.tensor_tensor(wplo[:], wp_st, wphi[:].bitcast(F32), ALU.subtract).then_inc(s["wp_lo"], 1)

            def embed(g, u, first, last):
                def place_patches(g, u):
                    dve.wait_ge(s["e_ps"], g + 1)
                    if not (fixed(g) and g < 2):
                        dve.wait_ge(s["e_tr"], g * 2 - 2)
                    for k in range(KD):
                        src = (S, R)[u][:, k * 512:k * 512 + GP].rearrange("p (b n) -> p b n", b=GSEQ)
                        i = nc.vector.tensor_tensor(emb[u][:, k, :, 1:1 + NPATCH], src,
                                                    posb[:, k:k + 1, :].to_broadcast([P, GSEQ, NPATCH]), ALU.add)
                    i.then_inc(s["e_emb"], 1)

                dve.wait_ge(s["ehi_done"], g + 1)
                nc.vector.tensor_tensor(elo[u][:], pst[u][:], ehi[u][:].bitcast(F32), ALU.subtract).then_inc(s["elo_done"], 1)
                if not first:
                    place_patches(g - 1, 1 - u)
                if last:
                    place_patches(g, u)

            chunks(dve, embed, G)
            dve.wait_ge(s["loaded"], 16 * N_LOADED)
            for m in range(KD):
                nc.vector.tensor_scalar(dmat[:, m, :], idt[:], dpt[:, m:m + 1], None, ALU.mult)
            nc.vector.tensor_copy(up[:], upf[:])
            nc.vector.tensor_copy(bvx[:], bvt[:].unsqueeze(2).to_broadcast([P, KD, L])).then_inc(s["set_dve"], 1)
            dve.wait_ge(s["set_pe"], 2)
            nc.vector.tensor_scalar(gam[:], R[:, 512:514], 1.0 / (D * F), QEPS, ALU.mult, ALU.add).then_inc(s["quant"], 1)
            dve.wait_ge(s["quant"], 3)
            nc.vector.reciprocal(ginv[:], gam[:]).then_inc(s["quant"], 1)
            dve.wait_ge(s["quant"], 4)
            n = 4
            for i, (w, wq) in enumerate(((w1st[:], w1q), (w2_st, w2q))):
                nc.vector.tensor_scalar(w, w, ginv[:, i:i + 1], ROUND, ALU.mult, ALU.add).then_inc(s["quant"], 1)
                dve.wait_ge(s["quant"], n + 1)
                nc.vector.tensor_scalar(w, w, ROUND, 1.0, ALU.subtract, ALU.min).then_inc(s["quant"], 1)
                dve.wait_ge(s["quant"], n + 2)
                ins = nc.vector.tensor_scalar(wq[:], w, -1.0, None, ALU.max)
                n += 2
            ins.then_inc(s["set_dve"], 1)
            dve.wait_ge(s["set_hi"], 1)
            for lo, src, hi in ((klo, k_st, khi), (qlo, q_st, qhi), (blo, b_st, bhi), (dlo, dmat[:], dhi),
                                (clo, c_st, chi), (vlo, banks(S, D), vhi)):
                ins = nc.vector.tensor_tensor(lo[:], src, hi[:].bitcast(F32), ALU.subtract)
            ins.then_inc(s["set_dve"], 1)

            dve.wait_ge(s["e_h"], 2 * G)
            ln_stats(dve, 0, 0)
            ln_norm(dve, 0, 0)
            ln_lo(dve, 0, 0)

            def rotate(c, z, z_done, half_done, dst, dst_done, first):
                def seqs(a):
                    return a.rearrange("p k (b l) -> p k b l", b=SEQ)

                dve.wait_ge(z_done, c + 1)
                full = [P, KD, SEQ, L]
                nc.vector.tensor_tensor(seqs(ra[:]), seqs(z[:]),
                                        cosT[:].unsqueeze(1).unsqueeze(1).to_broadcast(full), ALU.mult)
                for k in range(KD):
                    i = nc.vector.tensor_tensor(seqs(rb[:])[:, k], seqs(z[:])[:, 1 - k],
                                                sinT[:, k:k + 1, :].to_broadcast([P, SEQ, L]), ALU.mult)
                i.then_inc(half_done, 1)
                dve.wait_ge(half_done, c + 1)
                if not first:
                    dve.wait_ge(s["w_ps"], c)
                nc.vector.tensor_tensor(dst[:], ra[:], rb[:], ALU.add).then_inc(dst_done, 1)

            def attention(c, u, first, last):
                rotate(c, zk, s["zk_done"], s["rot_k"], kR, s["kR_done"], first)
                dve.wait_ge(s["kR_done"], c + 1)
                rotate(c, zq, s["zq_done"], s["rot_q"], qR, s["qR_done"], first)
                dve.wait_ge(s["v_ps"], c + 1)
                if not (fixed(c) and c < 2):
                    dve.wait_ge(s["ao_ps"], c - 1)
                nc.vector.tensor_tensor(vp[u][:], S[0:L, :].rearrange("p (b n) -> p b n", b=SEQ),
                                        bvp[:].unsqueeze(1).to_broadcast([L, SEQ, D]), ALU.add).then_inc(s["v_done"], 1)
                if not last:
                    ln_stats(dve, c + 1, c + 1)
                if not first:
                    add_back(dve, c - 1, s["a_tr"], s["a_res"])
                if not last:
                    ln_norm(dve, c + 1, c + 1)
                dve.wait_ge(s["w_ps"], c + 1)
                nc.vector.scalar_tensor_tensor(wm[:].rearrange("p (b l) -> p b l", b=SEQ),
                                               R[0:L, 0:T].rearrange("p (b l) -> p b l", b=SEQ), SCALE,
                                               msk[:].unsqueeze(1).to_broadcast([L, SEQ, L]),
                                               ALU.mult, ALU.add).then_inc(s["wm_done"], 1)
                dve.wait_ge(s["wl_done"], c + 1)
                nc.vector.scalar_tensor_tensor(wp[u][:], wm[:], 0.0, wl[:], ALU.max, ALU.add).then_inc(s["wp_done"], 1)
                if last:
                    add_back(dve, c, s["a_tr"], s["a_res"])
                    next_layer(NCH, s["a_res"])
                ln_lo(dve, c + 1, 1 - u)

            def next_layer(n, res):
                dve.wait_ge(res, NCH)
                ln_stats(dve, n, 0)
                ln_norm(dve, n, 0)

            chunks(dve, attention, NCH)

            def ffn(c, u, first, last):
                n = c + NCH

                def split(f):
                    dve.wait_ge(s["f_relu"], c * KF + f + 1)
                    nc.vector.tensor_tensor(hlo[:, f, :], rf[f % 4][:], hhi[:, f, :].bitcast(F32),
                                            ALU.subtract).then_inc(s["f_split"], 1)

                if not last:
                    ln_stats(dve, n + 1, c + 1)
                for f in range(4):
                    split(f)
                if not last:
                    ln_norm(dve, n + 1, c + 1)
                split(4)
                if not first:
                    add_back(dve, c - 1, s["f_tr"], s["f_res"])
                for f in range(5, KF):
                    split(f)
                if last:
                    add_back(dve, c, s["f_tr"], s["f_res"])
                    next_layer(2 * NCH, s["f_res"])
                ln_lo(dve, n + 1, 1 - u)

            chunks(dve, ffn, NCH)

            def ssm(c, u, first, last):
                n = c + 2 * NCH
                early = fixed(c) and c < 2
                dve.wait_ge(s["s_ps"], c + 1)
                if not early:
                    dve.wait_ge(s["s_lo"], c - 1)
                for b in range(SEQ):
                    bs = slice(b * L, (b + 1) * L)
                    i = nc.vector.tensor_tensor_scan(hs[u][:, bs], at[:], quarter[u][:, bs], 0.0, ALU.mult, ALU.add)
                i.then_inc(s["s_scan"], 1)
                if not last:
                    ln_stats(dve, n + 1, c + 1)
                if not early:
                    add_back(dve, c - 2, s["s_tr"], s["s_res"])
                dve.wait_ge(s["s_hi"], c + 1)
                nc.vector.tensor_tensor(slo[u][:], hs[u][:], shi[u][:].bitcast(F32), ALU.subtract).then_inc(s["s_lo"], 1)
                if not last:
                    ln_norm(dve, n + 1, c + 1)
                    ln_lo(dve, n + 1, 1 - u)
                else:
                    add_back(dve, c - 1, s["s_tr"], s["s_res"])
                    add_back(dve, c, s["s_tr"], s["s_res"])

            chunks(dve, ssm, NCH)

            dve.wait_ge(s["s_res"], NCH)

            def router(c, u, first, last):
                n = c + 3 * NCH
                ln_stats(dve, n - 0, c)
                dve.wait_ge(s["rstd_done"], n + 1)
                dve.wait_ge(s["xT_done"], n)
                for t in range(TPC):
                    i = nc.vector.tensor_scalar(xt[:, t, :], tiles(h, c)[:, t, :], mv[:, t, 0:1], rstd[:, t:t + 1],
                                                ALU.subtract, ALU.mult)
                i.then_inc(s["xn_done"], 1)
                for t in range(TPC):
                    i = nc.vector.tensor_scalar(tiles(rows, c)[:, t, 0:D], tiles(h, c)[:, t, :], mv[:, t, 0:1],
                                                rstd[:, t:t + 1], ALU.subtract, ALU.mult)

            chunks(dve, router, NCH)
            count = [0]

            def step(ins):
                count[0] += 1
                ins.then_inc(s["rt"], 1)
                dve.wait_ge(s["rt"], count[0])

            V = nc.vector
            full = [TT, NTILE, E]
            dve.wait_ge(s["lg_sb"], NCH)
            step(V.tensor_reduce(r1[0][:], lg[:], AX, ALU.max))
            step(V.tensor_tensor(r8[0][:], lg[:], r1[0][:].unsqueeze(2).to_broadcast(full), ALU.subtract))
            dve.wait_ge(s["rt_act"], 1)
            step(V.tensor_reduce(r1[1][:], r8[1][:], AX, ALU.add))
            step(V.reciprocal(r1[2][:], r1[1][:]))
            step(V.tensor_tensor(r8[0][:], r8[1][:], r1[2][:].unsqueeze(2).to_broadcast(full), ALU.mult))
            for choice in range(2):
                src = r8[0] if choice == 0 else r8[2]
                es = slice(choice * E, (choice + 1) * E)
                step(V.tensor_reduce(top[:, :, choice], src[:], AX, ALU.max))
                step(V.tensor_tensor(r8[1][:], src[:], top[:, :, choice:choice + 1].to_broadcast(full), ALU.is_equal))
                step(V.tensor_tensor(r8[1][:], r8[1][:], rev[:].unsqueeze(1).to_broadcast(full), ALU.mult))
                step(V.tensor_reduce(r1[0][:], r8[1][:], AX, ALU.max))
                step(V.tensor_tensor(m16[:, :, es], r8[1][:], r1[0][:].unsqueeze(2).to_broadcast(full), ALU.is_equal))
                if choice == 0:
                    step(V.scalar_tensor_tensor(r8[2][:], m16[:, :, es], 0.0, r8[0][:], ALU.is_equal, ALU.mult))
            assert count[0] == RT_CHOICES
            dve.wait_ge(s["rt_pe"], 1)
            step(V.tensor_scalar(cnt[:], X[0:TT, 0:G * E].rearrange("p (g e) -> p g e", g=G), float(CAP), None, ALU.min))
            for i in range(2):
                step(V.tensor_copy(p16[:, i * NTILE // 2:(i + 1) * NTILE // 2, :], before[i]))
            second = p16[:, :, E:].rearrange("p (g t) e -> p g t e", g=G)
            step(V.tensor_tensor(second, second, cnt[:].unsqueeze(2).to_broadcast([TT, G, TPG, E]), ALU.add))
            step(V.scalar_tensor_tensor(k16[:], p16[:], float(CAP), m16[:], ALU.is_lt, ALU.mult))
            step(V.tensor_reduce(t2[0][:], pair8(k16), AX, ALU.add))
            step(V.tensor_tensor(q16[:].rearrange("p (g t) e -> p g t e", g=G), p16[:].rearrange("p (g t) e -> p g t e", g=G),
                                 base[:].unsqueeze(2).to_broadcast([TT, G, TPG, 2 * E]), ALU.add))
            step(V.tensor_tensor(q16[:], q16[:], k16[:], ALU.mult))
            step(V.tensor_reduce(t2[1][:], pair8(q16), AX, ALU.add))
            step(V.tensor_tensor(t2[2][:], t2[0][:], top[:], ALU.mult))
            step(V.tensor_scalar(t2[3][:], t2[2][:], 0.0, None, ALU.not_equal))
            step(V.scalar_tensor_tensor(t2[1][:], t2[1][:], BIG, t2[3][:], ALU.subtract, ALU.mult))
            step(V.tensor_scalar(slot[:], t2[1][:], BIG, None, ALU.add))
            step(V.tensor_tensor(pair8(q16), pair8(k16), t2[2][:].unsqueeze(3).to_broadcast([TT, NTILE, 2, E]), ALU.mult))
            step(V.tensor_tensor(rows[:, :, D + 1:], q16[:, :, 0:E], q16[:, :, E:], ALU.add))
            step(V.tensor_copy(rows[:, :, D], tno[:]))
            assert count[0] == RT_ALL

            dve.sem_inc(s["hm_done"], NH)
            dve.sem_inc(s["mlo_done"], 1)
            dve.wait_ge(s["scattered"], 16 * 2 * NTILE)
            dve.wait_ge(s["h_out"], 16)

            def take_meta(e, j):
                dve.wait_ge(row_loaded[j], e * 32 + 32)
                dve.wait_ge(s["settled"], (e * NJ + j + 1) * ST)
                a, last = slot_tiles(CHUNKS[j][1])[0][1], slot_tiles(CHUNKS[j][1])[2][1]
                for n, ts in ((a, slice(0, 2)), (last, slice(2, 3))):
                    nc.vector.tensor_copy(tix[j][0:n, ts], gr[j][0:n, ts, D])
                    i = nc.vector.tensor_copy(gate[j][0:n, ts].unsqueeze(2), gr[j][0:n, ts, bass.ds(e + D + 1, 1)])
                i.then_inc(s["meta"], 1)

            def gx_split(j, q):
                n = CHUNKS[j][1]
                dve.wait_ge(s["gx_hi"], q + 1)
                nc.vector.tensor_tensor(gxlo[j][:, :, 0:n], banks(X, n), gxhi[j][:, :, 0:n].bitcast(F32),
                                        ALU.subtract).then_inc(s["gx_lo"], 1)

            def split_w(e, i):
                h0, hn = HT[i]
                dve.wait_ge(s["w_hi"], e * NH + i + 1)
                nc.vector.tensor_tensor(wlo[:, :, h0:h0 + hn], wst[:, :, h0:h0 + hn],
                                        whi[:, :, h0:h0 + hn].bitcast(F32), ALU.subtract).then_inc(s["w_lo"], 1)

            gx_split(0, 0)
            for i in range(NH):
                split_w(0, i)
            take_meta(0, 0)

            def expert(e, last):
                for j, (_, n) in enumerate(CHUNKS):
                    q = e * NJ + j

                    def hidden_lo(i):
                        hn = HT[i][1]
                        dve.wait_ge(s["mhi_done"], q * NH + i + 1)
                        nc.vector.tensor_tensor(mlo[0:hn, i, 0:n], hm[i % 2][0:hn, 0:n], mhi[0:hn, i, 0:n].bitcast(F32),
                                                ALU.subtract).then_inc(s["mlo_done"], 1)

                    for i, (h0, hn) in enumerate(HT):
                        dve.wait_ge(s["mlo_done"], q * NH + max(i, 1))
                        dve.wait_ge(s["gl_done"], q * NH + i + 1)
                        nc.vector.tensor_tensor(hm[i % 2][0:hn, 0:n], gl[i % 2][0:hn, 0:n],
                                                banks((S, R)[i % 2], n, hn)[:, 1, :], ALU.mult).then_inc(s["hm_done"], 1)
                        if i:
                            hidden_lo(i - 1)
                        if j == 0:
                            dve.wait_ge(s["wo_hi"], e * NH + i + 1)
                            nc.vector.tensor_tensor(wolo[0:hn, i, :], wost[0:hn, i, :], wohi[0:hn, i, :].bitcast(F32),
                                                    ALU.subtract).then_inc(s["wo_lo"], 1)
                        if j == NJ - 1 and not last:
                            split_w(e + 1, i)
                    hidden_lo(NH - 1)
                    if j < NJ - 1:
                        gx_split(j + 1, q + 1)
                        take_meta(e, j + 1)
                    elif not last:
                        gx_split(0, q + 1)
                        take_meta(e + 1, 0)

            with dve.Fori(0, E - 1) as e:
                expert(e, False)
            expert(E - 1, True)

        @block.gpsimd
        def _(pool):
            nc.gpsimd.memset(zrow, 0.0).then_inc(s["zero_ready"], 1)
            pool.wait_ge(s["zero_ready"], 1)
            nc.gpsimd.memset(zrow[:, D:D + 1], BIG).then_inc(s["zero_ready"], 1)
            pool.wait_ge(s["set_pool"], 4)

            def embed(g, u, first, last):
                pool.wait_ge(txt_loaded[u], (g - u) * 8 + 16 if not fixed(g) else 16 * (g // 2 + 1))
                if not (fixed(g) and g < 2):
                    pool.wait_ge(s["e_tr"], g * 2 - 2)
                stand_alone(pool)
                for k in range(KD):
                    i = nc.gpsimd.tensor_copy(emb[u][:, k, :, 1 + NPATCH:], tst[u][:, k])
                i.then_inc(s["e_txt"], 1)

            chunks(pool, embed, G)
            ln_rstd(pool, 0)
            with pool.Fori(1, 4 * NCH) as n:
                ln_rstd(pool, n)

            pool.wait_ge(s["rt"], RT_ALL)
            pool.wait_ge(s["xz_done"], 16)
            for t in range(NTILE):
                for choice in range(2):
                    pool.indirect_dma_start(out=xrows, out_offset=bass.IndirectOffsetOnAxis(slot[:, t, choice:choice + 1], 0),
                                            in_=rows[:, t, :], in_offset=None, bounds_check=NROW - 1,
                                            oob_is_err=False).then_inc(s["scattered"], 16)
            pool.sem_inc(s["settled"], ST * NJ)
            pool.wait_ge(s["h_out"], 16)

            def expert(e):
                for j, (_, n) in enumerate(CHUNKS):
                    for t, (a0, a) in enumerate(slot_tiles(n)):
                        r = (e * NJ + j) * ST + t
                        pool.wait_ge(s["y_sb"], r + 1 + ST)
                        stand_alone(pool)
                        pool.indirect_dma_start(out=out, out_offset=bass.IndirectOffsetOnAxis(tix[j][0:a, t:t + 1], 0),
                                                in_=ys[t][0:a, :], in_offset=None, bounds_check=NTOK - 1,
                                                oob_is_err=False, compute_op=ALU.add).then_inc(s["added"], 16)
                        pool.wait_ge(s["added"], (r + 1) * 16)
                        pool.sem_inc(s["settled"], 1)

            with pool.Fori(0, E) as e:
                expert(e)


def kernel(**inputs):
    import numpy as np
    import concourse.bacc as _bacc
    from concourse import mybir as _mybir
    from concourse.bass_utils import run_bass_kernel_spmd as _run

    a = {k: np.asarray(v) for k, v in inputs.items()}

    def cols(w):
        return w.reshape(-1, P, w.shape[-1]).transpose(1, 0, 2)

    def vec(b):
        return b.reshape(-1, P).T

    pairs = np.concatenate([np.arange(0, D, 2), np.arange(1, D, 2)])
    x = a["x"].reshape(G, GSEQ, 3, 6, 16, 6, 16).transpose(0, 2, 4, 6, 1, 3, 5)
    x = x.reshape(G, KP, P, GP).transpose(0, 2, 1, 3)
    txt = a["txt"].reshape(G, GSEQ, NTXT, KD, P).transpose(0, 4, 3, 1, 2)
    angle = np.outer(np.arange(L, dtype=np.float32), np.arange(P, dtype=np.float32))[::-1].astype(np.float64)
    cos, sin = np.cos(angle).T.astype(np.float32), np.sin(angle).T.astype(np.float32)
    j, i = np.meshgrid(np.arange(L), np.arange(L), indexing="ij")
    slotbase = np.arange(G)[:, None] * CAP + np.tile(np.arange(E), 2)[None] * SLOTS
    pos = a["L0_tok_pos_embed"][0]
    arrays = dict(
        patches=x, txt=txt,
        cls=vec(a["L0_tok_cls_token"].reshape(-1)), pos0=vec(pos[0]),
        pos=pos[1:].T.reshape(KD, P, NPATCH).transpose(1, 0, 2), tok_b=vec(a["L0_tok_b"]),
        w_patch=cols(a["L0_tok_W"].T),
        w_k=cols(a["L0_attn_Wk"][:, pairs]), w_q=cols(a["L0_attn_Wq"][:, pairs]),
        w_vT=cols(a["L0_attn_Wv"].T), w_p=cols(a["L0_attn_Wp"]),
        b_k=vec(a["L0_attn_bk"][pairs]), b_q=vec(a["L0_attn_bq"][pairs]),
        b_v=vec(a["L0_attn_bv"]), b_p=vec(a["L0_attn_bp"]),
        rot_cos=cos, rot_sin=np.stack([sin, -sin], 1),
        mask=np.where(j <= i, 0.0, MASKED).astype(np.float32),
        w1T=cols(a["L0_ffn_W1"].T), b1=vec(a["L0_ffn_b1"]), w2T=cols(a["L0_ffn_W2"].T), b2=vec(a["L0_ffn_b2"]),
        b_wT=cols(a["L1_attn_B_w"].T), c_wT=a["L1_attn_C_w"].T, log_a=a["L1_attn_log_A"][:, None],
        d_param=vec(a["L1_attn_D_param"]), w_r=cols(a["L1_ffn_router_w"]),
        w0=a["L1_ffn_w0_kernel"], w1=a["L1_ffn_w1_kernel"], wo=a["L1_ffn_wo_kernel"],
        ident=np.eye(P, dtype=np.float32), upper=np.triu(np.ones((TT, TT), np.float32), 1),
        tokno=np.arange(NTOK, dtype=np.float32).reshape(NTILE, TT).T,
        slotbase=np.broadcast_to(slotbase, (TT, G, 2 * E)).astype(np.float32),
        revno=np.broadcast_to(E - np.arange(E), (TT, E)).astype(np.float32),
    )
    arrays = {k: np.ascontiguousarray(v) for k, v in arrays.items()}
    nc = _bacc.Bacc("TRN2", target_bir_lowering=False, num_devices=1)
    args = {k: nc.dram_tensor(f"in_{k}", v.shape, _mybir.dt.from_np(v.dtype), kind="ExternalInput").ap()
            for k, v in arrays.items()}
    out = nc.dram_tensor("out_h", (NTOK, D), _mybir.dt.float32, kind="ExternalOutput").ap()
    fusion_kernel(nc, out=out, **args)
    r = _run(nc, [{f"in_{k}": v for k, v in arrays.items()}], core_ids=[0])
    return r.results[0]["out_h"].reshape(B, L, D)
```

```python
from contextlib import ExitStack

import concourse.bass as bass
from concourse import mybir

F32 = mybir.dt.float32
F32R = mybir.dt.float32r
BF16 = mybir.dt.bfloat16
U32 = mybir.dt.uint32
ALU = mybir.AluOpType
ACT = mybir.ActivationFunctionType
AX = mybir.AxisListType.X

P = 128
B = 64
NPATCH = 36
NTXT = 32
L = 1 + NPATCH + NTXT
D = 256
KD = D // P
NTOK = B * L
SEQ = 4
T = SEQ * L
NCH = B // SEQ
TT = 92
TPC = T // TT
NTILE = NTOK // TT
G = 8
TPG = NTILE // G
GSEQ = B // G
PD = 768
KP = PD // P
GP = GSEQ * NPATCH
F = 1024
KF = F // P
NS = 128
E = 8
CAP = 140
H = 1368
HT = [(i * P, min(P, H - i * P)) for i in range(-(-H // P))]
NH = len(HT)
SLOTS = G * CAP
CHUNKS = [(0, 374), (374, 374), (748, 372)]
NJ = len(CHUNKS)
NC = CHUNKS[0][1]
ST = 3
NROW = E * SLOTS
ROW = D + 1 + E
BIG = 65536.0
ROWS_PAD = 8600
EPS = 1e-5
QEPS = 1e-5
SCALE = float(D) ** -0.5
MASKED = -1e30
ROUND = 12582912.0


def slot_tiles(n):
    a = -(-n // ST)
    return [(0, a), (a, a), (2 * a, n - 2 * a)]


SMAX = slot_tiles(NC)[0][1]


def fixed(c):
    return isinstance(c, int)


def fusion_kernel(nc, patches, txt, cls, pos0, pos, tok_b, w_patch, w_k, w_q, w_vT, w_p, b_k, b_q, b_v, b_p,
                  rot_cos, rot_sin, mask, w1T, b1, w2T, b2, b_wT, c_wT, log_a, d_param, w_r,
                  w0, w1, wo, ident, upper, tokno, slotbase, revno, out):
    ctx = ExitStack()
    with ctx:
        def sem(name):
            return ctx.enter_context(nc.semaphore(name))

        def sbuf(stack, name, shape, dt=F32):
            return stack.enter_context(nc.sbuf_tensor(name, shape, dt))

        xrows = nc.dram_tensor("xrows", (NROW, ROW), F32).ap()

        idt = sbuf(ctx, "idt", [P, P])
        wst = sbuf(ctx, "wst", [P, 2 * KD, H])
        wost = sbuf(ctx, "wost", [P, NH, D])
        slot = sbuf(ctx, "slot", [TT, NTILE, 2], U32)

        pre = ExitStack()
        h = sbuf(pre, "h", [TT, NTILE, D])
        xt = sbuf(pre, "xt", [TT, TPC, D])
        xhi = [sbuf(pre, f"xhi{u}", [P, KD, T], F32R) for u in range(2)]
        xlo = [sbuf(pre, f"xlo{u}", [P, KD, T], F32R) for u in range(2)]
        oT = sbuf(pre, "oT", [P, KD, T])
        st = sbuf(pre, "st", [TT, TPC, 6])
        mv = sbuf(pre, "mv", [TT, TPC, 2])
        ve = sbuf(pre, "ve", [TT, TPC])
        rstd = sbuf(pre, "rstd", [TT, TPC])
        mhalf = sbuf(pre, "mhalf", [TT, TPC])
        epst = sbuf(pre, "epst", [TT, TPC])
        mone = sbuf(pre, "mone", [TT, TPC])
        mn = sbuf(pre, "mn", [TT, TPC])
        nb = sbuf(pre, "nb", [TT, TPC])
        bhi = sbuf(pre, "bhi", [P, KD, NS], F32R)
        blo = sbuf(pre, "blo", [P, KD, NS], F32R)
        chi = sbuf(pre, "chi", [P, D], F32R)
        clo = sbuf(pre, "clo", [P, D], F32R)
        dmat = sbuf(pre, "dmat", [P, KD, P])
        dhi = sbuf(pre, "dhi", [P, KD, P], F32R)
        dlo = sbuf(pre, "dlo", [P, KD, P], F32R)
        at = sbuf(pre, "at", [P, L])
        lat = sbuf(pre, "lat", [P, 1])
        dpt = sbuf(pre, "dpt", [P, KD])
        bkt = sbuf(pre, "bkt", [P, KD])
        bqt = sbuf(pre, "bqt", [P, KD])
        bvt = sbuf(pre, "bvt", [P, KD])
        bpt = sbuf(pre, "bpt", [P, KD])
        b1t = sbuf(pre, "b1t", [P, KF])
        b2t = sbuf(pre, "b2t", [P, KD])
        onesf = sbuf(pre, "onesf", [P, P])
        gsum = sbuf(pre, "gsum", [P, 2])
        gam = sbuf(pre, "gam", [P, 2])
        ginv = sbuf(pre, "ginv", [P, 2])
        wr = sbuf(pre, "wr", [P, KD, E])
        base = sbuf(pre, "base", [TT, G, 2 * E])
        rev = sbuf(pre, "rev", [TT, E])
        upf = sbuf(pre, "upf", [TT, TT])
        up = sbuf(pre, "up", [TT, TT], BF16)
        ones = sbuf(pre, "ones", [TT, TT], BF16)
        tno = sbuf(pre, "tno", [TT, NTILE])

        layers = ExitStack()
        w1st = sbuf(layers, "w1st", [P, KD, F])
        w1q = sbuf(layers, "w1q", [P, KD, F], F32R)
        w2q = sbuf(layers, "w2q", [P, KF, D], F32R)
        khi = sbuf(layers, "khi", [P, KD, D], F32R)
        klo = sbuf(layers, "klo", [P, KD, D], F32R)
        qhi = sbuf(layers, "qhi", [P, KD, D], F32R)
        qlo = sbuf(layers, "qlo", [P, KD, D], F32R)
        vhi = sbuf(layers, "vhi", [P, KD, D], F32R)
        vlo = sbuf(layers, "vlo", [P, KD, D], F32R)
        bvx = sbuf(layers, "bvx", [P, KD, L])
        bvp = sbuf(layers, "bvp", [L, D])
        cosT = sbuf(layers, "cosT", [P, L])
        sinT = sbuf(layers, "sinT", [P, KD, L])
        msk = sbuf(layers, "msk", [L, L])

        embed_ = ExitStack()
        pst = [sbuf(embed_, f"pst{u}", [P, KP, GP]) for u in range(2)]
        ehi = [sbuf(embed_, f"ehi{u}", [P, KP, GP], F32R) for u in range(2)]
        elo = [sbuf(embed_, f"elo{u}", [P, KP, GP], F32R) for u in range(2)]
        emb = [sbuf(embed_, f"emb{u}", [P, KD, GSEQ, L]) for u in range(2)]
        wphi = sbuf(embed_, "wphi", [P, KP, D], F32R)
        wplo = sbuf(embed_, "wplo", [P, KP, D], F32R)
        posb = sbuf(embed_, "posb", [P, KD, NPATCH])
        clst = sbuf(embed_, "clst", [P, KD])
        pos0t = sbuf(embed_, "pos0t", [P, KD])
        tokbt = sbuf(embed_, "tokbt", [P, KD])
        embed_.close()

        zk = sbuf(layers, "zk", [P, KD, T])
        zq = sbuf(layers, "zq", [P, KD, T])
        ra = [sbuf(layers, f"ra{i}", [P, KD, T]) for i in range(2)]
        rb = sbuf(layers, "rb", [P, KD, T])
        kR = sbuf(layers, "kR", [P, KD, T])
        qR = sbuf(layers, "qR", [P, KD, T])
        vp = [sbuf(layers, f"vp{u}", [L, SEQ, D]) for u in range(2)]
        wm = sbuf(layers, "wm", [L, T])
        wa = sbuf(layers, "wa", [L, T])
        we = sbuf(layers, "we", [L, T])
        wl = sbuf(layers, "wl", [L, T])
        wp = [sbuf(layers, f"wp{u}", [L, T]) for u in range(2)]
        hhi = sbuf(layers, "hhi", [P, KF, T], F32R)
        hlo = sbuf(layers, "hlo", [P, KF, T], F32R)
        rf = [sbuf(layers, f"rf{i}", [P, T]) for i in range(4)]
        layers.close()

        hs = [sbuf(pre, f"hs{u}", [P, T]) for u in range(2)]
        shi = [sbuf(pre, f"shi{u}", [P, T], F32R) for u in range(2)]
        slo = [sbuf(pre, f"slo{u}", [P, T], F32R) for u in range(2)]
        rxt = sbuf(pre, "rxt", [TT, TPC, D])
        rst = sbuf(pre, "rst", [TT, TPC, 6])
        rmv = sbuf(pre, "rmv", [TT, TPC, 2])
        rve = sbuf(pre, "rve", [TT, TPC])
        rrstd = sbuf(pre, "rrstd", [TT, TPC])
        rmn = sbuf(pre, "rmn", [TT, TPC])
        rnb = sbuf(pre, "rnb", [TT, TPC])
        xf = [sbuf(pre, f"xf{u}", [P, KD, T]) for u in range(2)]
        lg = sbuf(pre, "lg", [TT, TPG, E])
        r8 = [sbuf(pre, f"r8{i}", [TT, TPG, E]) for i in range(3)]
        m16 = sbuf(pre, "m16", [TT, TPG, 2 * E], BF16)
        p16 = sbuf(pre, "p16", [TT, TPG, 2 * E])
        k16 = sbuf(pre, "k16", [TT, TPG, 2 * E])
        q16 = sbuf(pre, "q16", [TT, TPG, 2 * E])
        cnt = sbuf(pre, "cnt", [TT, 1, E])
        r1 = [sbuf(pre, f"r1{i}", [TT, TPG]) for i in range(3)]
        top = sbuf(pre, "top", [TT, TPG, 2])
        t2 = [sbuf(pre, f"t2{i}", [TT, TPG, 2]) for i in range(4)]
        pad = sbuf(pre, "pad", [P, ROWS_PAD])
        rows = sbuf(pre, "rows", [TT, NTILE, ROW])
        pre.close()

        assert 4 * 4 * KD * H <= 4 * NTILE * D, "w0 and w1, split before the rows are dispatched, fit in the place of h"
        whi = sbuf(ctx, "whi", [P, 2 * KD, H], F32R)
        wlo = sbuf(ctx, "wlo", [P, 2 * KD, H], F32R)
        wohi = sbuf(ctx, "wohi", [P, NH, D], F32R)
        wolo = sbuf(ctx, "wolo", [P, NH, D], F32R)
        gxhi = [sbuf(ctx, f"gxhi{j}", [P, KD, NC], F32R) for j in range(NJ)]
        gxlo = [sbuf(ctx, f"gxlo{j}", [P, KD, NC], F32R) for j in range(NJ)]
        gr = [sbuf(ctx, f"gr{j}", [SMAX, ST, ROW]) for j in range(NJ)]
        gate = [sbuf(ctx, f"gate{j}", [SMAX, ST]) for j in range(NJ)]
        tix = [sbuf(ctx, f"tix{j}", [SMAX, ST], U32) for j in range(NJ)]
        gl = [sbuf(ctx, f"gl{i}", [P, NC]) for i in range(2)]
        hm = [sbuf(ctx, f"hm{i}", [P, NC]) for i in range(2)]
        mhi = sbuf(ctx, "mhi", [P, NH, NC], F32R)
        mlo = sbuf(ctx, "mlo", [P, NH, NC], F32R)
        ys = [sbuf(ctx, f"ys{i}", [SMAX, D]) for i in range(ST)]

        def psum(name):
            return ctx.enter_context(nc.psum_tensor(name, [P, 1024], F32))

        X, O, S, R = psum("X"), psum("O"), psum("S"), psum("R")

        def banks(t, n, m=P):
            return t[0:m, :].rearrange("p (k n) -> p k n", k=2)[:, :, 0:n]

        def tok3(t):
            return t[0:TT, 0:TPC * D].rearrange("p (t n) -> p t n", t=TPC)

        quarter = [S[:, 0:512], S[:, 512:1024], R[:, 0:512], R[:, 512:1024]]

        names = """first_loaded loaded gam_done ginv_done patch0 patch1 txt0 txt1 set_hi set_gam set_dve set_act set_pe set_pool zero_ready quant passed
        wp_hi wp_lo ehi_done elo_done e_ps e_emb e_txt e_tr e_h
        bn_done mv_done ve_done mn_done rstd_done nb_done xn_done xT_done hi_done lo_done
        k_ps q_ps v_ps zk_done zq_done rk_cos rq_cos rot_k rot_q kR_done qR_done v_done w_ps wm_done wa_done we_done wl_done
        wp_done ao_ps f_ps f_relu f_split f_down s_ps s_scan s_hi s_lo so_ps
        res_sb res_tr res_added
        h_out rbn_done rmv_done rve_done rrs_done rmn_done rnb_done rxn_done rows_done rxT_done rx_done
        lg_ps lg_taken tno_done rt rt_act rt_pe scattered0 scattered1 scattered2 xz_done
        w_load wo_load w_hi w_lo wo_hi wo_lo row0 row1 row2 gx_ps gx_hi gx_lo meta
        up_ps gl_done hm_done mhi_done mlo_done y_ps y_sb added settled""".split()
        s = {n: sem(n) for n in names}
        scattered = [s["scattered0"], s["scattered1"], s["scattered2"]]
        patch_loaded, txt_loaded, row_loaded = [s["patch0"], s["patch1"]], [s["txt0"], s["txt1"]], [s["row0"], s["row1"], s["row2"]]

        block = ctx.enter_context(nc.Block())

        def stand_alone(e):
            e.sem_inc(s["passed"], 1)

        def chunks(e, body, n, before_last=None):
            body(0, 0, True, False)
            body(1, 1, False, False)
            with e.Fori(1, n // 2 - 1) as i:
                body(i * 2, 0, False, False)
                body(i * 2 + 1, 1, False, False)
            if before_last:
                before_last()
            body(n - 2, 0, False, False)
            body(n - 1, 1, False, True)

        ROUTE, SCATTER, END = 6, 8, NCH + 6

        def pipeline(e, body, first, end):
            for c in range(first):
                body(c, c % 2, c // 2)
            with e.Fori(first // 2, NCH // 2 - 1) as i:
                body(i * 2, 0, i)
                body(i * 2 + 1, 1, i)
            for c in range(NCH - 2, end):
                body(c, c % 2, c // 2)

        def live(c, lag):
            return not fixed(c) or 0 <= c - lag < NCH

        def live_group(i, lag):
            return not fixed(i) or 0 <= i - lag < G

        def tiles(a, c, n=TPC):
            return a[:, c * n:(c + 1) * n, :] if fixed(c) else a[:, bass.ds(c * n, n), :]

        GPC = 3
        assert all(c0 + n <= GPC * (j + 1) * CAP for j, (c0, n) in enumerate(CHUNKS))
        N_FIRST, N_LOADED = 6, 24

        wflat = wst[:].rearrange("p a n -> p (a n)")
        oflat = wost[:].rearrange("p a n -> p (a n)")

        def wst_view(n, at_, k):
            return wst[:].rearrange("p a n -> p (a n)")[:, at_:at_ + n].rearrange("p (k n) -> p k n", k=k)

        wp_st = wst_view(KP * D, 0, KP)
        k_st, q_st, v_st, p_st = (wst_view(KD * D, KP * D + i * KD * D, KD) for i in range(4))
        c_st = wflat[:, 3584:3584 + D]
        b_st = wst_view(KD * NS, 3840, KD)
        w2_st = oflat[:, 0:KF * D].rearrange("p (k n) -> p k n", k=KF)
        zrow = wflat[:, 4096:4096 + ROW]
        tst = [wflat[:, 4400 + u * 512:4912 + u * 512].rearrange("p (k b n) -> p k b n", k=KD, b=GSEQ) for u in range(2)]

        state_ps = S[:, 0:T]
        logit_ps = S[0:TT, 512:512 + TPC * E].rearrange("p (t e) -> p t e", t=TPC)
        before = S[0:TT, 640:640 + TPG * 2 * E].rearrange("p (t e) -> p t e", e=2 * E)
        counts = S[0:TT, 768:768 + E]
        RT_CHOICES, RT_TAKEN, RT_ALL = 16, 18, 30

        def pair8(a):
            return a[:].rearrange("p t (c e) -> p t c e", c=2)

        def load_expert(sp, e):
            one = bass.ds(e, 1)
            for i, w in enumerate((w0, w1)):
                sp.dma_start(wst[:, i * KD:(i + 1) * KD, :],
                             w[one].rearrange("e (k p) h -> (e p) k h", p=P)).then_inc(s["w_load"], 16)
            full = NH - 1
            sp.dma_start(wost[:, 0:full, :],
                         wo[one, 0:full * P, :].rearrange("e (t p) n -> (e p) t n", p=P)).then_inc(s["wo_load"], 16)
            sp.dma_start(wost[0:HT[-1][1], full, :],
                         wo[one, full * P:H, :].rearrange("e p n -> (e p) n")).then_inc(s["wo_load"], 16)

        def load_rows(sp, e, j):
            c0, n = CHUNKS[j]
            a, last = slot_tiles(n)[0][1], slot_tiles(n)[2][1]
            ex = xrows.rearrange("(e r) n -> e r n", e=E)[bass.ds(e, 1)]
            sp.dma_start(gr[j][0:a, 0:2, :],
                         ex[:, c0:c0 + 2 * a, :].rearrange("e (t p) n -> (e p) t n", p=a)).then_inc(row_loaded[j], 16)
            sp.dma_start(gr[j][0:last, 2, :],
                         ex[:, c0 + 2 * a:c0 + n, :].rearrange("e p n -> (e p) n")).then_inc(row_loaded[j], 16)

        @block.sync
        def _(sp):
            for dst, src in ((idt[:], ident), (wst_view(1536, 0, KP), w_patch), (clst[:], cls), (pos0t[:], pos0),
                             (posb[:], pos), (tokbt[:], tok_b)):
                sp.dma_start(dst, src).then_inc(s["first_loaded"], 16)
            for g in range(2):
                sp.dma_start(pst[g][:], patches[g]).then_inc(patch_loaded[g], 16)
                sp.dma_start(tst[g], txt[g]).then_inc(txt_loaded[g], 16)

            def load_groups(i):
                for u in range(2):
                    g = i * 2 + u
                    one = slice(g, g + 1) if fixed(g) else bass.ds(g, 1)
                    sp.wait_ge(s["elo_done"], g - 1)
                    sp.dma_start(pst[u][:], patches[one].rearrange("a p b n -> (a p) b n")).then_inc(patch_loaded[u], 16)
                    sp.wait_ge(s["e_txt"], g - 1)
                    sp.dma_start(tst[u], txt[one].rearrange("a p k b n -> (a p) k b n")).then_inc(txt_loaded[u], 16)

            load_groups(1)
            for dst, src in (
                (k_st, w_k), (q_st, w_q), (v_st, w_vT), (p_st, w_p), (b_st, b_wT), (c_st, c_wT),
                (w1st[:], w1T), (w2_st, w2T), (bkt[:], b_k), (bqt[:], b_q), (bvt[:], b_v), (bpt[:], b_p),
                (b1t[:], b1), (b2t[:], b2), (lat[:], log_a), (dpt[:], d_param), (cosT[:], rot_cos),
                (sinT[:], rot_sin), (msk[:], mask), (wr[:], w_r), (base[:], slotbase),
            ):
                sp.dma_start(dst, src).then_inc(s["loaded"], 16)
            sp.dma_start(rev[:], revno).then_inc(s["loaded"], 16)
            sp.dma_start(upf[:], upper).then_inc(s["loaded"], 16)
            sp.dma_start(tno[:], tokno).then_inc(s["loaded"], 16)
            with sp.Fori(2, G // 2) as i:
                load_groups(i)
            sp.wait_ge(s["zero_ready"], 2)
            sp.dma_start(xrows.rearrange("(p a) n -> p a n", p=P),
                         zrow.unsqueeze(1).to_broadcast([P, NROW // P, ROW])).then_inc(s["xz_done"], 16)
            sp.wait_ge(s["xz_done"], 16)
            sp.wait_ge(s["set_dve"], 3)
            sp.wait_ge(s["set_pe"], 2)
            sp.wait_ge(s["quant"], 2 + 6 * KF)
            load_expert(sp, 0)
            with sp.Fori(0, NCH) as c:
                sp.wait_ge(s["res_added"], c + (2 * NCH + 1))
                sp.dma_start(out.rearrange("(t p) n -> p t n", p=TT)[:, bass.ds(c * TPC, TPC), :],
                             tiles(h, c)).then_inc(s["h_out"], 16)
            sp.wait_ge(s["h_out"], 16 * NCH)
            sp.wait_ge(s["rt"], G * RT_ALL)
            for j in range(NJ):
                sp.wait_ge(scattered[j], 16 * 2 * TPG * min(GPC, G - GPC * j))
                load_rows(sp, 0, j)
            with sp.Fori(0, E - 1) as e:
                sp.wait_ge(s["w_lo"], e * NH + NH)
                sp.wait_ge(s["wo_lo"], e * NH + NH)
                load_expert(sp, e + 1)
                for j in range(NJ):
                    sp.wait_ge(s["gx_ps"], e * NJ + j + 1)
                    sp.wait_ge(s["meta"], e * NJ + j + 1)
                    load_rows(sp, e + 1, j)
            sp.wait_ge(s["h_out"], 16 * NCH)
            sp.wait_ge(s["added"], 16 * ST * NJ * E)

        def ln_stats(dve, n, c):
            for t in range(TPC):
                i = nc.vector.bn_stats(st[:, t, :], tiles(h, c)[:, t, :])
            i.then_inc(s["bn_done"], 1)
            if not (fixed(n) and n == 0):
                dve.wait_ge(s["nb_done"], n)
            dve.wait_ge(s["bn_done"], n + 1)
            stand_alone(dve)
            for t in range(TPC):
                i = nc.vector.bn_aggr(mv[:, t, :], st[:, t, :])
            i.then_inc(s["mv_done"], 1)

        def ln_rstd(pool, n):
            pool.wait_ge(s["mv_done"], n + 1)
            nc.gpsimd.tensor_tensor(ve[:], mv[:, :, 1], epst[:], ALU.add).then_inc(s["ve_done"], 1)
            nc.gpsimd.tensor_tensor(mn[:], mv[:, :, 0], mone[:], ALU.mult).then_inc(s["mn_done"], 1)
            pool.wait_ge(s["ve_done"], n + 1)
            if not (fixed(n) and n == 0):
                pool.wait_ge(s["xn_done"], n)
            nc.gpsimd.tensor_tensor(rstd[:], ve[:], mhalf[:], ALU.pow).then_inc(s["rstd_done"], 1)
            pool.wait_ge(s["mn_done"], n + 1)
            pool.wait_ge(s["rstd_done"], n + 1)
            nc.gpsimd.tensor_tensor(nb[:], mn[:], rstd[:], ALU.mult).then_inc(s["nb_done"], 1)

        def ln_norm_act(act, n, c):
            act.wait_ge(s["nb_done"], n + 1)
            act.wait_ge(s["xT_done"], n)
            for t in range(TPC):
                i = nc.scalar.activation(xt[:, t, :], tiles(h, c)[:, t, :], ACT.Identity,
                                         scale=rstd[:, t:t + 1], bias=nb[:, t:t + 1])
            i.then_inc(s["xn_done"], 1)

        def ahead(c):
            return c if not fixed(c) or c < NCH else c - NCH

        def ln_norm(dve, n, c):
            dve.wait_ge(s["rstd_done"], n + 1)
            if not (fixed(n) and n == 0):
                dve.wait_ge(s["xT_done"], n)
            for t in range(TPC):
                i = nc.vector.tensor_scalar(xt[:, t, :], tiles(h, c)[:, t, :], mv[:, t, 0:1], rstd[:, t:t + 1],
                                            ALU.subtract, ALU.mult)
            i.then_inc(s["xn_done"], 1)

        def ln_transpose(pe, n):
            pe.wait_ge(s["xn_done"], n + 1)
            for t in range(TPC):
                for k in range(KD):
                    i = nc.tensor.transpose(banks(X, T)[:, k, t * TT:(t + 1) * TT], xt[:, t, k * P:(k + 1) * P],
                                            idt[0:TT, 0:TT])
            i.then_inc(s["xT_done"], 1)

        def ln_hi(act, n, u):
            act.wait_ge(s["xT_done"], n + 1)
            nc.scalar.activation(xhi[u][:], banks(X, T), ACT.Copy).then_inc(s["hi_done"], 1)

        def ln_lo(dve, n, u):
            dve.wait_ge(s["hi_done"], n + 1)
            nc.vector.tensor_tensor(xlo[u][:], banks(X, T), xhi[u][:].bitcast(F32), ALU.subtract).then_inc(s["lo_done"], 1)

        def add_back(dve, r, c):
            dve.wait_ge(s["res_tr"], r + 1)
            nc.vector.tensor_tensor(tiles(h, c), tiles(h, c), tok3(X), ALU.add).then_inc(s["res_added"], 1)

        def back_transpose(pe, r, n):
            pe.wait_ge(s["res_sb"], r + 1)
            pe.wait_ge(s["lo_done"], n + 1)
            for t in range(TPC):
                for k in range(KD):
                    i = nc.tensor.transpose(tok3(X)[:, t, k * P:(k + 1) * P], oT[:, k, t * TT:(t + 1) * TT], idt[:])
            i.then_inc(s["res_tr"], 1)

        def mm3(o, ahi, alo, xh, xl, start, stop):
            nc.tensor.matmul(o, ahi, xh, start=start, stop=False)
            nc.tensor.matmul(o, ahi, xl, start=False, stop=False)
            return nc.tensor.matmul(o, alo, xh, start=False, stop=stop)

        @block.tensor
        def _(pe):
            pe.wait_ge(s["wp_lo"], 1)
            pe.wait_ge(s["first_loaded"], 16 * N_FIRST)

            def embed_back(g, u, gfirst):
                pe.wait_ge(s["e_emb"], g + 1)
                pe.wait_ge(s["e_txt"], g + 1)
                for c, dst in enumerate((X, O)):
                    if not gfirst:
                        pe.wait_ge(s["e_h"], g * 2 + c - 1)
                    for t in range(TPC):
                        for k in range(KD):
                            em = emb[u][:, k].rearrange("p b l -> p (b l)")
                            i = nc.tensor.transpose(tok3(dst)[:, t, k * P:(k + 1) * P],
                                                    em[:, c * T + t * TT:c * T + (t + 1) * TT], idt[:])
                    i.then_inc(s["e_tr"], 1)

            def embed(g, u, first, last):
                pe.wait_ge(s["elo_done"], g + 1)
                if not (fixed(g) and g < 2):
                    pe.wait_ge(s["e_emb"], g - 1)
                for m in range(KD):
                    for k in range(KP):
                        i = mm3(banks((S, R)[u], GP)[:, m, :], wphi[:, k, m * P:(m + 1) * P],
                                wplo[:, k, m * P:(m + 1) * P], ehi[u][:, k, :], elo[u][:, k, :], k == 0, k == KP - 1)
                i.then_inc(s["e_ps"], 1)
                if not first:
                    embed_back(g - 1, 1 - u, fixed(g) and g == 1)
                if last:
                    embed_back(g, u, False)

            chunks(pe, embed, G)
            pe.wait_ge(s["loaded"], 16 * N_LOADED)
            pe.wait_ge(s["set_dve"], 1)
            for m in range(KD):
                for k in range(KD):
                    nc.tensor.matmul(S[:, m * 512:m * 512 + D], v_st[:, k, m * P:(m + 1) * P], p_st[:, k, :],
                                     start=k == 0, stop=k == KD - 1)
            for k in range(KD):
                i = nc.tensor.matmul(R[0:L, 0:D], bvx[:, k, :], p_st[:, k, :], start=k == 0, stop=k == KD - 1)
            i.then_inc(s["set_pe"], 1)
            pe.wait_ge(s["set_gam"], 2)
            nc.tensor.matmul(R[:, 512:514], onesf[:], gsum[:], start=True, stop=True).then_inc(s["set_pe"], 1)

            pe.wait_ge(s["set_dve"], 3)
            pe.wait_ge(s["set_act"], 1)
            pe.wait_ge(s["e_h"], 2 * G)
            ln_transpose(pe, 0)

            def weighted_sum(c, u, cfirst):
                pe.wait_ge(s["wp_done"], c + 1)
                if not cfirst:
                    pe.wait_ge(s["res_sb"], c)
                for b in range(SEQ):
                    for m in range(KD):
                        i = nc.tensor.matmul(banks(O, T)[:, m, b * L:(b + 1) * L], vp[u][:, b, m * P:(m + 1) * P],
                                             wp[u][:, b * L:(b + 1) * L], start=True, stop=True)
                i.then_inc(s["ao_ps"], 1)

            def attention(c, u, first, last):
                pe.wait_ge(s["lo_done"], c + 1)
                if not first:
                    pe.wait_ge(s["v_done"], c)
                for dst, hi, lo, done in ((S, khi, klo, s["k_ps"]), (R, qhi, qlo, s["q_ps"])):
                    if dst is R and not first:
                        pe.wait_ge(s["wm_done"], c)
                    for m in range(KD):
                        for k in range(KD):
                            i = mm3(banks(dst, T)[:, m, :], hi[:, k, m * P:(m + 1) * P], lo[:, k, m * P:(m + 1) * P],
                                    xhi[u][:, k, :], xlo[u][:, k, :], k == 0, k == KD - 1)
                    i.then_inc(done, 1)
                if not (fixed(c) and c < 2):
                    pe.wait_ge(s["res_added"], c - 1)
                ln_transpose(pe, c + 1)
                pe.wait_ge(s["zk_done"], c + 1)
                for b in range(SEQ):
                    for k in range(KD):
                        xs = slice(b * L, (b + 1) * L)
                        o = S[0:L, b * D:(b + 1) * D]
                        nc.tensor.matmul(o, xhi[u][:, k, xs], vhi[:, k, :], start=k == 0, stop=False)
                        nc.tensor.matmul(o, xhi[u][:, k, xs], vlo[:, k, :], start=False, stop=False)
                        i = nc.tensor.matmul(o, xlo[u][:, k, xs], vhi[:, k, :], start=False, stop=k == KD - 1)
                i.then_inc(s["v_ps"], 1)
                if not first:
                    weighted_sum(c - 1, 1 - u, fixed(c) and c == 1)
                pe.wait_ge(s["qR_done"], c + 1)
                for b in range(SEQ):
                    bs = slice(b * L, (b + 1) * L)
                    for k in range(KD):
                        i = nc.tensor.matmul(R[0:L, bs], qR[:, k, bs], kR[:, k, bs], start=k == 0, stop=k == KD - 1)
                i.then_inc(s["w_ps"], 1)
                if not first:
                    back_transpose(pe, c - 1, c + 1)
                if last:
                    weighted_sum(c, u, False)
                    pe.wait_ge(s["res_added"], c)
                    back_transpose(pe, c, c + 1)

            chunks(pe, attention, NCH)

            def down(c, f):
                pe.wait_ge(s["f_split"], c * KF + f + 1)
                if f == 0:
                    pe.wait_ge(s["res_sb"], NCH + c)
                for m in range(KD):
                    w = w2q[:, f, m * P:(m + 1) * P]
                    nc.tensor.matmul(banks(O, T)[:, m, :], w, hhi[:, f, :], start=f == 0, stop=False)
                    i = nc.tensor.matmul(banks(O, T)[:, m, :], w, hlo[:, f, :], start=False, stop=f == KF - 1)
                i.then_inc(s["f_down"], 1)

            def ffn(c, u, first, last):
                n = c + NCH
                pe.wait_ge(s["lo_done"], n + 1)
                for f in range(KF):
                    if f >= 4 or not first:
                        pe.wait_ge(s["f_relu"], c * KF + f - 3)
                    o = quarter[f % 4][:, 0:T]
                    for k in range(KD):
                        w = w1q[:, k, f * P:(f + 1) * P]
                        nc.tensor.matmul(o, w, xhi[u][:, k, :], start=k == 0, stop=False)
                        i = nc.tensor.matmul(o, w, xlo[u][:, k, :], start=False, stop=k == KD - 1)
                    i.then_inc(s["f_ps"], 1)
                    if f == 1:
                        pe.wait_ge(s["res_added"], NCH if fixed(c) and c < 2 else NCH + c - 2)
                        ln_transpose(pe, n + 1)
                    if f and not first:
                        down(c - 1, f - 1)
                    if f == 4 and not (fixed(c) and c < 2):
                        back_transpose(pe, NCH + c - 2, n + 1)
                if not first:
                    down(c - 1, KF - 1)
                if last:
                    for f in range(KF):
                        down(c, f)
                        if f == 0:
                            pe.wait_ge(s["res_added"], NCH + c - 1)
                            back_transpose(pe, NCH + c - 1, n + 1)
                    pe.wait_ge(s["res_added"], NCH + c)
                    back_transpose(pe, NCH + c, n + 1)

            pe.wait_ge(s["quant"], 2 + 6 * KF)
            chunks(pe, ffn, NCH)

            def skip_term(c, u):
                pe.wait_ge(s["res_sb"], 2 * NCH + c)
                for m in range(KD):
                    mm3(banks(O, T)[:, m, :], dhi[:, m, :], dlo[:, m, :], xhi[u][:, m, :], xlo[u][:, m, :], True, False)

            def state_term(c, u):
                pe.wait_ge(s["s_lo"], c + 1)
                for m in range(KD):
                    ms = slice(m * P, (m + 1) * P)
                    i = mm3(banks(O, T)[:, m, :], chi[:, ms], clo[:, ms], shi[u][:], slo[u][:], False, True)
                i.then_inc(s["so_ps"], 1)

            def router_transpose(c):
                pe.wait_ge(s["rxn_done"], c + 1)
                if not (fixed(c) and c == 0):
                    pe.wait_ge(s["rx_done"], c)
                for t in range(TPC):
                    for k in range(KD):
                        i = nc.tensor.transpose(banks(R, T)[:, k, t * TT:(t + 1) * TT], rxt[:, t, k * P:(k + 1) * P],
                                                idt[0:TT, 0:TT])
                i.then_inc(s["rxT_done"], 1)

            def logits(c, u):
                pe.wait_ge(s["rx_done"], c + 1)
                if not (fixed(c) and c == 0):
                    pe.wait_ge(s["lg_taken"], c)
                for t in range(TPC):
                    for k in range(KD):
                        i = nc.tensor.matmul(logit_ps[:, t, :], xf[u][:, k, t * TT:(t + 1) * TT], wr[:, k, :],
                                             start=k == 0, stop=k == KD - 1)
                i.then_inc(s["lg_ps"], 1)

            def count_tokens(g):
                pe.wait_ge(s["rt"], g * RT_ALL + RT_CHOICES)
                nc.tensor.matmul(before, up[:], m16[:], start=True, stop=False)
                for t in range(TPG - 1):
                    n = TPG - 1 - t
                    nc.tensor.matmul(before[:, t + 1:, :], ones[:], m16[:, t:t + 1, :].to_broadcast([TT, n, 2 * E]),
                                     start=False, stop=t == TPG - 2)
                for t in range(TPG):
                    i = nc.tensor.matmul(counts, ones[:], m16[:, t, 0:E], start=t == 0, stop=t == TPG - 1)
                i.then_inc(s["rt_pe"], 1)

            def ssm(c, u, half):
                n = c + 2 * NCH
                if live(c, -1):
                    pe.wait_ge(s["res_added"], 2 * NCH if fixed(c) and c < 2 else 2 * NCH + c - 2)
                    ln_transpose(pe, n + 1)
                if live(c, 0):
                    pe.wait_ge(s["lo_done"], n + 1)
                    if not (fixed(c) and c == 0):
                        pe.wait_ge(s["s_scan"], c)
                    for k in range(KD):
                        i = mm3(state_ps, bhi[:, k, :], blo[:, k, :], xhi[u][:, k, :], xlo[u][:, k, :],
                                k == 0, k == KD - 1)
                    i.then_inc(s["s_ps"], 1)
                if live(c, 1):
                    state_term(c - 1, 1 - u)
                if live(c, 2):
                    if not live(c, -1):
                        pe.wait_ge(s["res_added"], 2 * NCH + c - 2)
                    back_transpose(pe, 2 * NCH + c - 2, n + 1 if live(c, -1) else 3 * NCH - 1)
                if u == 1 and live_group(half, ROUTE // 2):
                    if live(c, 5):
                        pe.wait_ge(s["lg_taken"], c - 4)
                    count_tokens(half - ROUTE // 2)
                if live(c, 0):
                    skip_term(c, u)
                if live(c, 4):
                    if u == 1 and live_group(half, ROUTE // 2):
                        pe.wait_ge(s["rt"], (half - ROUTE // 2) * RT_ALL + RT_TAKEN)
                    logits(c - 4, u)
                if live(c, 3):
                    router_transpose(c - 3)

            pipeline(pe, ssm, ROUTE, END)

            def gx_transpose(e, j, first):
                pe.wait_ge(row_loaded[j], e * 32 + 32)
                if not first:
                    pe.wait_ge(s["gx_lo"], e * NJ + j)
                n = CHUNKS[j][1]
                for t, (a0, a) in enumerate(slot_tiles(n)):
                    for k in range(KD):
                        i = nc.tensor.transpose(banks(X, n)[:, k, a0:a0 + a], gr[j][0:a, t, k * P:(k + 1) * P],
                                                idt[0:a, 0:a])
                i.then_inc(s["gx_ps"], 1)

            pe.wait_ge(s["rt"], G * RT_ALL)
            pe.sem_inc(s["y_ps"], 1)
            gx_transpose(0, 0, True)

            def expert(e, last):
                for j, (_, n) in enumerate(CHUNKS):
                    q = e * NJ + j
                    pe.wait_ge(s["gx_lo"], q + 1)
                    for i, (h0, hn) in enumerate(HT):
                        if j == 0:
                            pe.wait_ge(s["w_lo"], e * NH + i + 1)
                        pe.wait_ge(s["hm_done"], q * NH + (NH + i - 1 if i else NH))
                        for w in range(2):
                            for k in range(KD):
                                ins = mm3(banks((S, R)[i % 2], n, hn)[:, w, :], whi[:, w * KD + k, h0:h0 + hn],
                                          wlo[:, w * KD + k, h0:h0 + hn], gxhi[j][:, k, 0:n], gxlo[j][:, k, 0:n],
                                          k == 0, k == KD - 1)
                        ins.then_inc(s["up_ps"], 1)
                    if j < NJ - 1:
                        gx_transpose(e, j + 1, False)
                    elif not last:
                        gx_transpose(e + 1, 0, False)
                    for t, (a0, a) in enumerate(slot_tiles(n)):
                        pe.wait_ge(s["y_sb"], q * ST + (ST, ST - 1, ST + 1)[t])
                        o = O[0:a, (t % 2) * 512:(t % 2) * 512 + D]
                        for i, (h0, hn) in enumerate(HT):
                            if t == 0:
                                pe.wait_ge(s["mlo_done"], q * NH + i + 2)
                                if j == 0:
                                    pe.wait_ge(s["wo_lo"], e * NH + i + 1)
                            lh, ll = mhi[0:hn, i, a0:a0 + a], mlo[0:hn, i, a0:a0 + a]
                            nc.tensor.matmul(o, lh, wohi[0:hn, i, :], start=i == 0, stop=False)
                            nc.tensor.matmul(o, lh, wolo[0:hn, i, :], start=False, stop=False)
                            ins = nc.tensor.matmul(o, ll, wohi[0:hn, i, :], start=False, stop=i == NH - 1)
                        ins.then_inc(s["y_ps"], 1)

            with pe.Fori(0, E - 1) as e:
                expert(e, False)
            expert(E - 1, True)

        @block.scalar
        def _(act):
            act.preload_act_table_set("natural_log_exp_and_others")
            act.wait_ge(s["first_loaded"], 16 * N_FIRST)
            nc.scalar.activation(wphi[:], wp_st, ACT.Copy).then_inc(s["wp_hi"], 1)

            def embed_out(g):
                for c, src in enumerate((X, O)):
                    act.wait_ge(s["e_tr"], g * 2 + c + 1)
                    nc.scalar.activation(tiles(h, g * 2 + c), tok3(src), ACT.Copy).then_inc(s["e_h"], 1)

            def embed(g, u, first, last):
                act.wait_ge(patch_loaded[u], (g - u) * 8 + 16 if not fixed(g) else 16 * (g // 2 + 1))
                if not (fixed(g) and g < 2):
                    act.wait_ge(s["e_ps"], g - 1)
                nc.scalar.activation(ehi[u][:], pst[u][:], ACT.Copy).then_inc(s["ehi_done"], 1)
                if not (fixed(g) and g < 2):
                    embed_out(g - 2)
                if last:
                    embed_out(g - 1)
                    embed_out(g)

            def split_weights():
                act.wait_ge(s["loaded"], 16 * N_LOADED)
                act.wait_ge(s["set_dve"], 1)
                for dst, src in ((khi, k_st), (qhi, q_st), (bhi, b_st), (dhi, dmat[:])):
                    nc.scalar.activation(dst[:], src, ACT.Copy)
                nc.scalar.activation(chi[:], c_st, ACT.Copy).then_inc(s["set_hi"], 1)
                nc.scalar.activation(w1q[:], w1st[:], ACT.Abs, accum_out=gsum[:, 0:1]).then_inc(s["set_gam"], 1)
                nc.scalar.activation(w2q[:], w2_st, ACT.Abs, accum_out=gsum[:, 1:2]).then_inc(s["set_gam"], 1)
                nc.scalar.activation(at[:], lat[:].to_broadcast([P, L]), ACT.Exp).then_inc(s["set_act"], 1)

            chunks(act, embed, G, split_weights)
            act.wait_ge(s["set_pe"], 1)
            nc.scalar.activation(vhi[:], banks(S, D), ACT.Copy)
            nc.scalar.activation(bvp[:], R[0:L, 0:D], ACT.Copy).then_inc(s["set_hi"], 1)

            ln_hi(act, 0, 0)

            def result(r, src_done, count, bias):
                act.wait_ge(src_done, count)
                if not (fixed(r) and r == 0):
                    act.wait_ge(s["res_tr"], r)
                if bias is None:
                    i = nc.scalar.activation(oT[:], banks(O, T), ACT.Copy)
                else:
                    for m in range(KD):
                        i = nc.scalar.activation(oT[:, m, :], banks(O, T)[:, m, :], ACT.Identity, bias=bias[:, m:m + 1])
                i.then_inc(s["res_sb"], 1)

            def log_term(c):
                act.wait_ge(s["wm_done"], c + 1)
                if not (fixed(c) and c == 0):
                    act.wait_ge(s["wp_done"], c)
                nc.scalar.activation(wa[:], wm[:], ACT.Abs).then_inc(s["wa_done"], 1)
                act.wait_ge(s["wa_done"], c + 1)
                nc.scalar.activation(we[:], wa[:], ACT.Exp, scale=-1.0).then_inc(s["we_done"], 1)
                act.wait_ge(s["we_done"], c + 1)
                nc.scalar.activation(wl[:], we[:], ACT.Ln, bias=1.0).then_inc(s["wl_done"], 1)

            def attention(c, u, first, last):
                for z, src, bias, ps_done, z_done, rot in (
                        (zk, S, bkt, s["k_ps"], s["zk_done"], s["kR_done"]), (zq, R, bqt, s["q_ps"], s["zq_done"], s["qR_done"])):
                    act.wait_ge(ps_done, c + 1)
                    if not first:
                        act.wait_ge(rot, c)
                    for m in range(KD):
                        i = nc.scalar.activation(z[:, m, :], banks(src, T)[:, m, :], ACT.Identity, bias=bias[:, m:m + 1])
                    i.then_inc(z_done, 1)
                    if z is zk and not first:
                        log_term(c - 1)
                ln_hi(act, c + 1, 1 - u)
                ln_norm_act(act, c + 2, ahead(c + 2))
                if not first:
                    result(c - 1, s["ao_ps"], c, bpt)
                if last:
                    log_term(c)
                    result(c, s["ao_ps"], c + 1, bpt)

            chunks(act, attention, NCH)

            def ffn(c, u, first, last):
                n = c + NCH
                if not (fixed(c) and c < 2):
                    result(NCH + c - 2, s["f_down"], (c - 1) * KF, b2t)
                for f in range(KF):
                    act.wait_ge(s["f_ps"], c * KF + f + 1)
                    if f >= 4 or not first:
                        act.wait_ge(s["f_split"], c * KF + f - 3)
                    nc.scalar.activation(rf[f % 4][:], quarter[f % 4][:, 0:T], ACT.Relu, bias=b1t[:, f:f + 1])
                    if not first:
                        act.wait_ge(s["f_down"], (c - 1) * KF + f + 1)
                    nc.scalar.activation(hhi[:, f, :], quarter[f % 4][:, 0:T], ACT.Relu,
                                         bias=b1t[:, f:f + 1]).then_inc(s["f_relu"], 1)
                    if f == 1:
                        ln_hi(act, n + 1, 1 - u)
                if last:
                    result(NCH + c - 1, s["f_down"], c * KF, b2t)
                    result(NCH + c, s["f_down"], (c + 1) * KF, b2t)

            chunks(act, ffn, NCH)

            def split_w(e, i):
                h0, hn = HT[i]
                nc.scalar.activation(whi[:, :, h0:h0 + hn], wst[:, :, h0:h0 + hn], ACT.Copy).then_inc(s["w_hi"], 1)

            def ssm(c, u, half):
                n = c + 2 * NCH
                def router_norm(dst, done):
                    for t in range(TPC):
                        i = nc.scalar.activation(dst[:, t, :], tiles(h, c - 3)[:, t, :], ACT.Identity,
                                                 scale=rrstd[:, t:t + 1], bias=rnb[:, t:t + 1])
                    i.then_inc(done, 1)

                if live(c, -1):
                    ln_hi(act, n + 1, 1 - u)
                if live(c, 4):
                    act.wait_ge(s["rxT_done"], c - 3)
                    if not (fixed(c) and c < 6):
                        act.wait_ge(s["lg_ps"], c - 5)
                    nc.scalar.activation(xf[u][:], banks(R, T), ACT.Copy).then_inc(s["rx_done"], 1)
                if live(c, 0):
                    act.wait_ge(s["s_scan"], c + 1)
                    if not (fixed(c) and c < 2):
                        act.wait_ge(s["so_ps"], c - 1)
                    nc.scalar.activation(shi[u][:], hs[u][:], ACT.Copy).then_inc(s["s_hi"], 1)
                if live(c, 1):
                    result(2 * NCH + c - 1, s["so_ps"], c, None)
                if u == 0 and live_group(half, ROUTE // 2):
                    g = half - ROUTE // 2
                    act.wait_ge(s["rt"], g * RT_ALL + 2)
                    nc.scalar.activation(r8[1][:], r8[0][:], ACT.Exp).then_inc(s["rt_act"], 1)
                if live(c, 3):
                    act.wait_ge(s["rnb_done"], c - 2)
                    if not (fixed(c) and c == 3):
                        act.wait_ge(s["rxT_done"], c - 3)
                    router_norm(rxt[:], s["rxn_done"])
                if live(c, -2):
                    ln_norm_act(act, n + 2, c + 2)
                if live(c, 3):
                    router_norm(tiles(rows, c - 3)[:, :, 0:D], s["rows_done"])

                if fixed(c) and c == NCH + 3:
                    act.wait_ge(s["h_out"], 16 * NCH)
                    act.wait_ge(s["rmv_done"], NCH)
                    act.wait_ge(s["w_load"], 32)
                    for i in range(NH // 2):
                        split_w(0, i)
                if fixed(c) and c == NCH + 4:
                    for i in range(NH // 2, NH):
                        split_w(0, i)

            pipeline(act, ssm, ROUTE, END)

            act.wait_ge(s["rt"], G * RT_ALL)
            act.sem_inc(s["y_sb"], ST)
            act.wait_ge(s["gx_ps"], 1)
            nc.scalar.activation(gxhi[0][:, :, 0:CHUNKS[0][1]], banks(X, CHUNKS[0][1]), ACT.Copy).then_inc(s["gx_hi"], 1)

            def expert(e, last):
                for j, (_, n) in enumerate(CHUNKS):
                    q = e * NJ + j

                    def hidden_hi(i):
                        hn = HT[i][1]
                        act.wait_ge(s["hm_done"], q * NH + i + 1 + NH)
                        nc.scalar.activation(mhi[0:hn, i, 0:n], hm[i % 2][0:hn, 0:n], ACT.Copy).then_inc(s["mhi_done"], 1)

                    if j == 0:
                        act.wait_ge(s["wo_load"], e * 32 + 32)
                    if j == NJ - 1 and not last:
                        act.wait_ge(s["w_load"], e * 32 + 64)
                    for i, (h0, hn) in enumerate(HT):
                        act.wait_ge(s["up_ps"], q * NH + i + 1)
                        act.wait_ge(s["hm_done"], q * NH + i - 1 + NH)
                        nc.scalar.activation(gl[i % 2][0:hn, 0:n], banks((S, R)[i % 2], n, hn)[:, 0, :],
                                             ACT.Gelu_apprx_tanh).then_inc(s["gl_done"], 1)
                        if i == 0:
                            act.wait_ge(s["y_ps"], q * ST + 1)
                        if i:
                            hidden_hi(i - 1)
                        if j == 0:
                            nc.scalar.activation(wohi[0:hn, i, :], wost[0:hn, i, :], ACT.Copy).then_inc(s["wo_hi"], 1)
                        if j == NJ - 1 and not last:
                            split_w(e + 1, i)
                    hidden_hi(NH - 1)
                    if not (last and j == NJ - 1):
                        nn = CHUNKS[(j + 1) % NJ][1]
                        act.wait_ge(s["gx_ps"], q + 2)
                        nc.scalar.activation(gxhi[(j + 1) % NJ][:, :, 0:nn], banks(X, nn), ACT.Copy).then_inc(s["gx_hi"], 1)
                    for t, (a0, a) in enumerate(slot_tiles(n)):
                        act.wait_ge(s["y_ps"], q * ST + t + 2)
                        act.wait_ge(s["meta"], q + 1)
                        act.wait_ge(s["settled"], q * ST + t - ST + 1 + ST * NJ)
                        nc.scalar.activation(ys[t][0:a, :], O[0:a, (t % 2) * 512:(t % 2) * 512 + D], ACT.Copy,
                                             scale=gate[j][0:a, t:t + 1]).then_inc(s["y_sb"], 1)

            with act.Fori(0, E - 1) as e:
                expert(e, False)
            expert(E - 1, True)

        @block.vector
        def _(dve):
            nc.vector.memset(mhalf[:], -0.5).then_inc(s["set_pool"], 1)
            nc.vector.memset(epst[:], EPS).then_inc(s["set_pool"], 1)
            nc.vector.memset(mone[:], -1.0).then_inc(s["set_pool"], 1)
            nc.vector.memset(onesf[:], 1.0).then_inc(s["set_pool"], 1)
            nc.vector.memset(ones[:], 1.0).then_inc(s["set_pool"], 1)
            dve.wait_ge(s["first_loaded"], 16 * N_FIRST)
            nc.vector.tensor_tensor(clst[:], clst[:], pos0t[:], ALU.add).then_inc(s["quant"], 1)
            nc.vector.tensor_tensor(posb[:], posb[:], tokbt[:].unsqueeze(2).to_broadcast([P, KD, NPATCH]),
                                    ALU.add).then_inc(s["quant"], 1)
            dve.wait_ge(s["quant"], 2)
            for u in range(2):
                for k in range(KD):
                    nc.vector.tensor_copy(emb[u][:, k, :, 0], clst[:, k:k + 1].to_broadcast([P, GSEQ]))
            dve.wait_ge(s["wp_hi"], 1)
            nc.vector.tensor_tensor(wplo[:], wp_st, wphi[:].bitcast(F32), ALU.subtract).then_inc(s["wp_lo"], 1)

            def embed(g, u, first, last):
                def place_patches(g, u):
                    dve.wait_ge(s["e_ps"], g + 1)
                    if not (fixed(g) and g < 2):
                        dve.wait_ge(s["e_tr"], g * 2 - 2)
                    for k in range(KD):
                        src = (S, R)[u][:, k * 512:k * 512 + GP].rearrange("p (b n) -> p b n", b=GSEQ)
                        i = nc.vector.tensor_tensor(emb[u][:, k, :, 1:1 + NPATCH], src,
                                                    posb[:, k:k + 1, :].to_broadcast([P, GSEQ, NPATCH]), ALU.add)
                    i.then_inc(s["e_emb"], 1)

                dve.wait_ge(s["ehi_done"], g + 1)
                nc.vector.tensor_tensor(elo[u][:], pst[u][:], ehi[u][:].bitcast(F32), ALU.subtract).then_inc(s["elo_done"], 1)
                if not first:
                    place_patches(g - 1, 1 - u)
                if last:
                    place_patches(g, u)

            def split_weights():
                dve.wait_ge(s["loaded"], 16 * N_LOADED)
                for m in range(KD):
                    nc.vector.tensor_scalar(dmat[:, m, :], idt[:], dpt[:, m:m + 1], None, ALU.mult)
                nc.vector.tensor_copy(up[:], upf[:])
                nc.vector.tensor_copy(bvx[:], bvt[:].unsqueeze(2).to_broadcast([P, KD, L])).then_inc(s["set_dve"], 1)
                dve.wait_ge(s["set_hi"], 1)
                for lo, src, hi in ((klo, k_st, khi), (qlo, q_st, qhi), (blo, b_st, bhi), (dlo, dmat[:], dhi), (clo, c_st, chi)):
                    i = nc.vector.tensor_tensor(lo[:], src, hi[:].bitcast(F32), ALU.subtract)
                i.then_inc(s["set_dve"], 1)

            chunks(dve, embed, G, split_weights)
            dve.wait_ge(s["e_h"], 1)
            ln_stats(dve, 0, 0)
            dve.wait_ge(s["set_hi"], 2)
            nc.vector.tensor_tensor(vlo[:], banks(S, D), vhi[:].bitcast(F32), ALU.subtract).then_inc(s["set_dve"], 1)
            dve.wait_ge(s["set_pe"], 2)
            nc.vector.tensor_scalar(gam[:], R[:, 512:514], 1.0 / (D * F), QEPS, ALU.mult, ALU.add).then_inc(s["gam_done"], 1)
            dve.wait_ge(s["gam_done"], 1)
            nc.vector.reciprocal(ginv[:], gam[:]).then_inc(s["ginv_done"], 1)

            ln_norm(dve, 0, 0)
            ln_lo(dve, 0, 0)
            ln_stats(dve, 1, 1)
            ln_norm(dve, 1, 1)

            def rotate(c, z, i, z_done, cos_done, half_done, dst, dst_done, first):
                def seqs(a):
                    return a.rearrange("p k (b l) -> p k b l", b=SEQ)

                dve.wait_ge(z_done, c + 1)
                for k in range(KD):
                    ins = nc.vector.tensor_tensor(seqs(rb[:])[:, k], seqs(z[:])[:, 1 - k],
                                                  sinT[:, k:k + 1, :].to_broadcast([P, SEQ, L]), ALU.mult)
                ins.then_inc(half_done, 1)
                dve.wait_ge(half_done, c + 1)
                dve.wait_ge(cos_done, c + 1)
                if not first:
                    dve.wait_ge(s["w_ps"], c)
                nc.vector.tensor_tensor(dst[:], ra[i][:], rb[:], ALU.add).then_inc(dst_done, 1)

            def softplus(c, u):
                dve.wait_ge(s["wl_done"], c + 1)
                nc.vector.scalar_tensor_tensor(wp[u][:], wm[:], 0.0, wl[:], ALU.max, ALU.add).then_inc(s["wp_done"], 1)

            def attention(c, u, first, last):
                ln_stats(dve, c + 2, ahead(c + 2))
                rotate(c, zk, 0, s["zk_done"], s["rk_cos"], s["rot_k"], kR, s["kR_done"], first)
                if not first:
                    softplus(c - 1, 1 - u)
                dve.wait_ge(s["kR_done"], c + 1)
                rotate(c, zq, 1, s["zq_done"], s["rq_cos"], s["rot_q"], qR, s["qR_done"], first)
                ln_lo(dve, c + 1, 1 - u)
                dve.wait_ge(s["v_ps"], c + 1)
                if not (fixed(c) and c < 2):
                    dve.wait_ge(s["ao_ps"], c - 1)
                nc.vector.tensor_tensor(vp[u][:], S[0:L, :].rearrange("p (b n) -> p b n", b=SEQ),
                                        bvp[:].unsqueeze(1).to_broadcast([L, SEQ, D]), ALU.add).then_inc(s["v_done"], 1)
                dve.wait_ge(s["w_ps"], c + 1)
                nc.vector.scalar_tensor_tensor(wm[:].rearrange("p (b l) -> p b l", b=SEQ),
                                               R[0:L, 0:T].rearrange("p (b l) -> p b l", b=SEQ), SCALE,
                                               msk[:].unsqueeze(1).to_broadcast([L, SEQ, L]),
                                               ALU.mult, ALU.add).then_inc(s["wm_done"], 1)
                if not first:
                    add_back(dve, c - 1, c - 1)
                if last:
                    softplus(c, u)
                    add_back(dve, c, c)

            chunks(dve, attention, NCH)

            def ffn(c, u, first, last):
                n = c + NCH

                def split(f):
                    dve.wait_ge(s["f_relu"], c * KF + f + 1)
                    nc.vector.tensor_tensor(hlo[:, f, :], rf[f % 4][:], hhi[:, f, :].bitcast(F32),
                                            ALU.subtract).then_inc(s["f_split"], 1)

                split(0)
                split(1)
                ln_lo(dve, n + 1, 1 - u)
                split(2)
                ln_stats(dve, n + 2, ahead(c + 2))
                split(3)
                split(4)
                if not (fixed(c) and c < 2):
                    add_back(dve, NCH + c - 2, c - 2)
                split(5)
                ln_norm(dve, n + 2, ahead(c + 2))
                split(6)
                split(7)
                if last:
                    add_back(dve, NCH + c - 1, c - 1)
                    add_back(dve, NCH + c, c)

            chunks(dve, ffn, NCH)

            V = nc.vector
            full = [TT, TPG, E]

            def step(g, k, ins, after=None):
                ins.then_inc(s["rt"], 1)
                dve.wait_ge(s["rt"], g * RT_ALL + (k if after is None else after))
                return k + 1

            def less_max(g):
                k = step(g, 1, V.tensor_reduce(r1[0][:], lg[:], AX, ALU.max))
                step(g, k, V.tensor_tensor(r8[0][:], lg[:], r1[0][:].unsqueeze(2).to_broadcast(full), ALU.subtract))

            def choose(g):
                dve.wait_ge(s["rt_act"], g + 1)
                k = step(g, 3, V.tensor_reduce(r1[1][:], r8[1][:], AX, ALU.add))
                k = step(g, k, V.reciprocal(r1[2][:], r1[1][:]))
                k = step(g, k, V.tensor_tensor(r8[0][:], r8[1][:], r1[2][:].unsqueeze(2).to_broadcast(full), ALU.mult))
                for choice in range(2):
                    src = r8[0] if choice == 0 else r8[2]
                    best, m = top[:, :, choice:choice + 1], m16[:, :, choice * E:(choice + 1) * E]
                    k = step(g, k, V.tensor_reduce(top[:, :, choice], src[:], AX, ALU.max))
                    k = step(g, k, V.tensor_tensor(r8[1][:], src[:], best.to_broadcast(full), ALU.is_equal))
                    k = step(g, k, V.tensor_tensor(r8[1][:], r8[1][:], rev[:].unsqueeze(1).to_broadcast(full), ALU.mult))
                    k = step(g, k, V.tensor_reduce(r1[0][:], r8[1][:], AX, ALU.max))
                    k = step(g, k, V.tensor_tensor(m, r8[1][:], r1[0][:].unsqueeze(2).to_broadcast(full), ALU.is_equal))
                    if choice == 0:
                        k = step(g, k, V.scalar_tensor_tensor(r8[2][:], m, 0.0, r8[0][:], ALU.is_equal, ALU.mult))
                assert k == RT_CHOICES + 1

            def take_counts(g):
                dve.wait_ge(s["rt_pe"], g + 1)
                k = step(g, RT_CHOICES + 1, V.tensor_scalar(cnt[:, 0, :], counts, float(CAP), None, ALU.min))
                step(g, k, V.tensor_copy(p16[:], before))

            def place(g):
                one = slice(g, g + 1) if fixed(g) else bass.ds(g, 1)
                k = RT_TAKEN + 1
                second = p16[:, :, E:]
                k = step(g, k, V.tensor_tensor(second, second, cnt[:].to_broadcast(full), ALU.add))
                k = step(g, k, V.scalar_tensor_tensor(k16[:], p16[:], float(CAP), m16[:], ALU.is_lt, ALU.mult), k - 1)
                k = step(g, k, V.tensor_tensor(q16[:], p16[:], base[:, one, :].to_broadcast([TT, TPG, 2 * E]), ALU.add), k - 1)
                k = step(g, k, V.tensor_reduce(t2[0][:], pair8(k16), AX, ALU.add), k - 1)
                k = step(g, k, V.tensor_tensor(q16[:], q16[:], k16[:], ALU.mult), k - 1)
                k = step(g, k, V.tensor_tensor(t2[2][:], t2[0][:], top[:], ALU.mult), k - 1)
                k = step(g, k, V.tensor_reduce(t2[1][:], pair8(q16), AX, ALU.add), k - 1)
                k = step(g, k, V.tensor_scalar(t2[3][:], t2[2][:], 0.0, None, ALU.not_equal), k - 1)
                k = step(g, k, V.tensor_tensor(pair8(q16), pair8(k16), t2[2][:].unsqueeze(3).to_broadcast([TT, TPG, 2, E]),
                                               ALU.mult), k - 1)
                k = step(g, k, V.scalar_tensor_tensor(t2[1][:], t2[1][:], BIG, t2[3][:], ALU.subtract, ALU.mult), k - 1)
                k = step(g, k, V.tensor_tensor(tiles(rows, g, TPG)[:, :, D + 1:], q16[:, :, 0:E], q16[:, :, E:], ALU.add), k - 1)
                k = step(g, k, V.tensor_scalar(tiles(slot, g, TPG), t2[1][:], BIG, None, ALU.add))
                assert k == RT_ALL + 1

            nc.vector.tensor_copy(rows[:, :, D], tno[:]).then_inc(s["tno_done"], 1)

            def split_w(e, i):
                h0, hn = HT[i]
                dve.wait_ge(s["w_hi"], e * NH + i + 1)
                nc.vector.tensor_tensor(wlo[:, :, h0:h0 + hn], wst[:, :, h0:h0 + hn],
                                        whi[:, :, h0:h0 + hn].bitcast(F32), ALU.subtract).then_inc(s["w_lo"], 1)

            EARLY = 3

            def ssm(c, u, half):
                n = c + 2 * NCH
                g = half - ROUTE // 2
                if live(c, -2):
                    ln_stats(dve, n + 2, c + 2)
                if live(c, -1):
                    ln_lo(dve, n + 1, 1 - u)
                if live(c, 0):
                    dve.wait_ge(s["s_ps"], c + 1)
                    if not (fixed(c) and c < 2):
                        dve.wait_ge(s["s_lo"], c - 1)
                    for b in range(SEQ):
                        bs = slice(b * L, (b + 1) * L)
                        i = nc.vector.tensor_tensor_scan(hs[u][:, bs], at[:], state_ps[:, bs], 0.0, ALU.mult, ALU.add)
                    i.then_inc(s["s_scan"], 1)
                if live(c, 5):
                    dve.wait_ge(s["lg_ps"], c - 4)
                    nc.vector.tensor_copy(lg[:, (1 - u) * TPC:(2 - u) * TPC, :], logit_ps).then_inc(s["lg_taken"], 1)
                if u == 0 and live_group(half, ROUTE // 2):
                    dve.wait_ge(s["lg_taken"], c - 4)
                    less_max(g)
                    if fixed(c) and c == NCH + 4:
                        split_w(0, 0)
                if live(c, 0):
                    dve.wait_ge(s["s_hi"], c + 1)
                    nc.vector.tensor_tensor(slo[u][:], hs[u][:], shi[u][:].bitcast(F32), ALU.subtract).then_inc(s["s_lo"], 1)
                if live(c, 2):
                    add_back(dve, 2 * NCH + c - 2, c - 2)
                if fixed(c) and c == NCH + 5:
                    for i in range(1, EARLY):
                        split_w(0, i)
                if u == 1 and live_group(half, ROUTE // 2):
                    take_counts(g)
                if live(c, 2):
                    dve.wait_ge(s["res_added"], 2 * NCH + c - 1)
                    stand_alone(dve)
                    for t in range(TPC):
                        i = nc.vector.bn_stats(rst[:, t, :], tiles(h, c - 2)[:, t, :])
                    i.then_inc(s["rbn_done"], 1)
                    if not (fixed(c) and c == 2):
                        dve.wait_ge(s["rnb_done"], c - 2)
                    dve.wait_ge(s["rbn_done"], c - 1)
                    stand_alone(dve)
                    for t in range(TPC):
                        i = nc.vector.bn_aggr(rmv[:, t, :], rst[:, t, :])
                    i.then_inc(s["rmv_done"], 1)
                if live_group(half, ROUTE // 2):
                    (choose, place)[u](g)

            pipeline(dve, ssm, ROUTE + 2, END)

            dve.sem_inc(s["hm_done"], NH)
            dve.sem_inc(s["mlo_done"], 1)

            def take_meta(e, j):
                dve.wait_ge(row_loaded[j], e * 32 + 32)
                dve.wait_ge(s["settled"], (e * NJ + j + 1) * ST)
                a, last = slot_tiles(CHUNKS[j][1])[0][1], slot_tiles(CHUNKS[j][1])[2][1]
                for n, ts in ((a, slice(0, 2)), (last, slice(2, 3))):
                    nc.vector.tensor_copy(tix[j][0:n, ts], gr[j][0:n, ts, D])
                    i = nc.vector.tensor_copy(gate[j][0:n, ts].unsqueeze(2), gr[j][0:n, ts, bass.ds(e + D + 1, 1)])
                i.then_inc(s["meta"], 1)

            def gx_split(j, q):
                n = CHUNKS[j][1]
                dve.wait_ge(s["gx_hi"], q + 1)
                nc.vector.tensor_tensor(gxlo[j][:, :, 0:n], banks(X, n), gxhi[j][:, :, 0:n].bitcast(F32),
                                        ALU.subtract).then_inc(s["gx_lo"], 1)

            for i in range(EARLY, NH):
                split_w(0, i)
            gx_split(0, 0)
            take_meta(0, 0)

            def expert(e, last):
                for j, (_, n) in enumerate(CHUNKS):
                    q = e * NJ + j

                    def hidden_lo(i):
                        hn = HT[i][1]
                        dve.wait_ge(s["mhi_done"], q * NH + i + 1)
                        nc.vector.tensor_tensor(mlo[0:hn, i, 0:n], hm[i % 2][0:hn, 0:n], mhi[0:hn, i, 0:n].bitcast(F32),
                                                ALU.subtract).then_inc(s["mlo_done"], 1)

                    for i, (h0, hn) in enumerate(HT):
                        dve.wait_ge(s["mlo_done"], q * NH + max(i, 1))
                        dve.wait_ge(s["gl_done"], q * NH + i + 1)
                        nc.vector.tensor_tensor(hm[i % 2][0:hn, 0:n], gl[i % 2][0:hn, 0:n],
                                                banks((S, R)[i % 2], n, hn)[:, 1, :], ALU.mult).then_inc(s["hm_done"], 1)
                        if i:
                            hidden_lo(i - 1)
                        if j == 0:
                            dve.wait_ge(s["wo_hi"], e * NH + i + 1)
                            nc.vector.tensor_tensor(wolo[0:hn, i, :], wost[0:hn, i, :], wohi[0:hn, i, :].bitcast(F32),
                                                    ALU.subtract).then_inc(s["wo_lo"], 1)
                        if j == NJ - 1 and not last:
                            split_w(e + 1, i)
                    hidden_lo(NH - 1)
                    if j < NJ - 1:
                        gx_split(j + 1, q + 1)
                        take_meta(e, j + 1)
                    elif not last:
                        gx_split(0, q + 1)
                        take_meta(e + 1, 0)

            with dve.Fori(0, E - 1) as e:
                expert(e, False)
            expert(E - 1, True)

        @block.gpsimd
        def _(pool):
            nc.gpsimd.memset(zrow, 0.0).then_inc(s["zero_ready"], 1)
            pool.wait_ge(s["zero_ready"], 1)
            nc.gpsimd.memset(zrow[:, D:D + 1], BIG).then_inc(s["zero_ready"], 1)
            pool.wait_ge(s["set_pool"], 5)

            def embed(g, u, first, last):
                pool.wait_ge(txt_loaded[u], (g - u) * 8 + 16 if not fixed(g) else 16 * (g // 2 + 1))
                if not (fixed(g) and g < 2):
                    pool.wait_ge(s["e_tr"], g * 2 - 2)
                stand_alone(pool)
                for k in range(KD):
                    i = nc.gpsimd.tensor_copy(emb[u][:, k, :, 1 + NPATCH:], tst[u][:, k])
                i.then_inc(s["e_txt"], 1)

            chunks(pool, embed, G)
            ln_rstd(pool, 0)
            ln_rstd(pool, 1)

            def ternary(k, f):
                n = f * 6 + (k * 3 + 2)
                if k:
                    w, wq = w2_st[:, f, :], w2q[:, f, :]
                else:
                    w, wq = w1st[:, :, f * P:(f + 1) * P], w1q[:, :, f * P:(f + 1) * P]
                nc.gpsimd.tensor_scalar(w, w, ginv[:, k:k + 1], ROUND, ALU.mult, ALU.add).then_inc(s["quant"], 1)
                pool.wait_ge(s["quant"], n + 1)
                nc.gpsimd.tensor_scalar(w, w, ROUND, 1.0, ALU.subtract, ALU.min).then_inc(s["quant"], 1)
                pool.wait_ge(s["quant"], n + 2)
                nc.gpsimd.tensor_scalar(wq, w, -1.0, None, ALU.max).then_inc(s["quant"], 1)

            def cosines(c, i):
                z, z_done, dst_done, cos_done = ((zk, s["zk_done"], s["kR_done"], s["rk_cos"]),
                                                 (zq, s["zq_done"], s["qR_done"], s["rq_cos"]))[i]
                pool.wait_ge(z_done, c + 1)
                if c:
                    pool.wait_ge(dst_done, c)
                nc.gpsimd.tensor_tensor(ra[i][:].rearrange("p k (b l) -> p k b l", b=SEQ),
                                        z[:].rearrange("p k (b l) -> p k b l", b=SEQ),
                                        cosT[:].unsqueeze(1).unsqueeze(1).to_broadcast([P, KD, SEQ, L]),
                                        ALU.mult).then_inc(cos_done, 1)

            for c in range(NCH):
                cosines(c, 0)
                ln_rstd(pool, c + 2)
                cosines(c, 1)
                if c == 0:
                    pool.wait_ge(s["ginv_done"], 1)
                ternary(c % 2, c // 2)
            with pool.Fori(NCH + 2, 2 * NCH + 2) as n:
                ln_rstd(pool, n)

            pool.wait_ge(s["xz_done"], 16)
            pool.wait_ge(s["tno_done"], 1)

            def ssm(c, u, half):
                def dispatch(choice):
                    if live_group(half, SCATTER // 2):
                        g = half - SCATTER // 2
                        pool.wait_ge(s["rt"], (g + 1) * RT_ALL)
                        pool.wait_ge(s["rows_done"], g * 2 + 2)
                        for t in range(TPC):
                            k = g * TPG + (u * TPC + t)
                            pool.indirect_dma_start(out=xrows, out_offset=bass.IndirectOffsetOnAxis(slot[:, k, choice:choice + 1], 0),
                                                    in_=rows[:, k, :], in_offset=None, bounds_check=NROW - 1,
                                                    oob_is_err=False).then_inc(scattered[g // GPC], 16)

                if live(c, -2):
                    ln_rstd(pool, c + (2 * NCH + 2))
                dispatch(0)
                if live(c, 2):
                    m = c - 2
                    pool.wait_ge(s["rmv_done"], m + 1)
                    if not (fixed(m) and m == 0):
                        pool.wait_ge(s["rows_done"], m)
                    nc.gpsimd.tensor_tensor(rve[:], rmv[:, :, 1], epst[:], ALU.add).then_inc(s["rve_done"], 1)
                    nc.gpsimd.tensor_tensor(rmn[:], rmv[:, :, 0], mone[:], ALU.mult).then_inc(s["rmn_done"], 1)
                    pool.wait_ge(s["rve_done"], m + 1)
                    nc.gpsimd.tensor_tensor(rrstd[:], rve[:], mhalf[:], ALU.pow).then_inc(s["rrs_done"], 1)
                    pool.wait_ge(s["rmn_done"], m + 1)
                    pool.wait_ge(s["rrs_done"], m + 1)
                    nc.gpsimd.tensor_tensor(rnb[:], rmn[:], rrstd[:], ALU.mult).then_inc(s["rnb_done"], 1)
                dispatch(1)

            for c in range(END + 2):
                ssm(c, c % 2, c // 2)

            pool.sem_inc(s["settled"], ST * NJ)
            pool.wait_ge(s["h_out"], 16 * NCH)

            def expert(e):
                for j, (_, n) in enumerate(CHUNKS):
                    for t, (a0, a) in enumerate(slot_tiles(n)):
                        r = (e * NJ + j) * ST + t
                        pool.wait_ge(s["y_sb"], r + 1 + ST)
                        stand_alone(pool)
                        pool.indirect_dma_start(out=out, out_offset=bass.IndirectOffsetOnAxis(tix[j][0:a, t:t + 1], 0),
                                                in_=ys[t][0:a, :], in_offset=None, bounds_check=NTOK - 1,
                                                oob_is_err=False, compute_op=ALU.add).then_inc(s["added"], 16)
                        pool.wait_ge(s["added"], (r + 1) * 16)
                        pool.sem_inc(s["settled"], 1)

            with pool.Fori(0, E) as e:
                expert(e)


def kernel(**inputs):
    import numpy as np
    import concourse.bacc as _bacc
    from concourse import mybir as _mybir
    from concourse.bass_utils import run_bass_kernel_spmd as _run

    a = {k: np.asarray(v) for k, v in inputs.items()}

    def cols(w):
        return w.reshape(-1, P, w.shape[-1]).transpose(1, 0, 2)

    def vec(b):
        return b.reshape(-1, P).T

    pairs = np.concatenate([np.arange(0, D, 2), np.arange(1, D, 2)])
    x = a["x"].reshape(G, GSEQ, 3, 6, 16, 6, 16).transpose(0, 2, 4, 6, 1, 3, 5)
    x = x.reshape(G, KP, P, GP).transpose(0, 2, 1, 3)
    txt = a["txt"].reshape(G, GSEQ, NTXT, KD, P).transpose(0, 4, 3, 1, 2)
    angle = np.outer(np.arange(L, dtype=np.float32), np.arange(P, dtype=np.float32))[::-1].astype(np.float64)
    cos, sin = np.cos(angle).T.astype(np.float32), np.sin(angle).T.astype(np.float32)
    j, i = np.meshgrid(np.arange(L), np.arange(L), indexing="ij")
    slotbase = np.arange(G)[:, None] * CAP + np.tile(np.arange(E), 2)[None] * SLOTS
    pos = a["L0_tok_pos_embed"][0]
    arrays = dict(
        patches=x, txt=txt,
        cls=vec(a["L0_tok_cls_token"].reshape(-1)), pos0=vec(pos[0]),
        pos=pos[1:].T.reshape(KD, P, NPATCH).transpose(1, 0, 2), tok_b=vec(a["L0_tok_b"]),
        w_patch=cols(a["L0_tok_W"].T),
        w_k=cols(a["L0_attn_Wk"][:, pairs]), w_q=cols(a["L0_attn_Wq"][:, pairs]),
        w_vT=cols(a["L0_attn_Wv"].T), w_p=cols(a["L0_attn_Wp"]),
        b_k=vec(a["L0_attn_bk"][pairs]), b_q=vec(a["L0_attn_bq"][pairs]),
        b_v=vec(a["L0_attn_bv"]), b_p=vec(a["L0_attn_bp"]),
        rot_cos=cos, rot_sin=np.stack([sin, -sin], 1),
        mask=np.where(j <= i, 0.0, MASKED).astype(np.float32),
        w1T=cols(a["L0_ffn_W1"].T), b1=vec(a["L0_ffn_b1"]), w2T=cols(a["L0_ffn_W2"].T), b2=vec(a["L0_ffn_b2"]),
        b_wT=cols(a["L1_attn_B_w"].T), c_wT=a["L1_attn_C_w"].T, log_a=a["L1_attn_log_A"][:, None],
        d_param=vec(a["L1_attn_D_param"]), w_r=cols(a["L1_ffn_router_w"]),
        w0=a["L1_ffn_w0_kernel"], w1=a["L1_ffn_w1_kernel"], wo=a["L1_ffn_wo_kernel"],
        ident=np.eye(P, dtype=np.float32), upper=np.triu(np.ones((TT, TT), np.float32), 1),
        tokno=np.arange(NTOK, dtype=np.float32).reshape(NTILE, TT).T,
        slotbase=np.broadcast_to(slotbase, (TT, G, 2 * E)).astype(np.float32),
        revno=np.broadcast_to(E - np.arange(E), (TT, E)).astype(np.float32),
    )
    arrays = {k: np.ascontiguousarray(v) for k, v in arrays.items()}
    nc = _bacc.Bacc("TRN2", target_bir_lowering=False, num_devices=1)
    args = {k: nc.dram_tensor(f"in_{k}", v.shape, _mybir.dt.from_np(v.dtype), kind="ExternalInput").ap()
            for k, v in arrays.items()}
    out = nc.dram_tensor("out_h", (NTOK, D), _mybir.dt.float32, kind="ExternalOutput").ap()
    fusion_kernel(nc, out=out, **args)
    r = _run(nc, [{f"in_{k}": v for k, v in arrays.items()}], core_ids=[0])
    return r.results[0]["out_h"].reshape(B, L, D)
```
